# Optimizing a Trainium2 kernel written in Bass

```python
import numpy as np
import jax
import jax.numpy as jnp

def _softmax(x, axis=-1):
    return jax.nn.softmax(x, axis=axis)

def _gelu(x):
    return jax.nn.gelu(x, approximate=True)

def _silu(x):
    return jax.nn.silu(x)

def _sigmoid(x):
    return jax.nn.sigmoid(x)

def _layernorm(x, axis=-1, eps=1e-05):
    m = jnp.mean(x, axis=axis, keepdims=True)
    v = jnp.var(x, axis=axis, keepdims=True)
    return (x - m) / jnp.sqrt(v + eps)

def _scatter_add(tgt, idx, src, axis=0):
    return tgt.at[idx].add(src)

def _segment_sum(src, seg, n):
    return jax.ops.segment_sum(src, seg, n)
kernel_name = 'mk_gnn_preln_d4_gnn_r32_5d1252'

def setup_inputs(seed: int=0):
    np.random.seed(seed)
    _w = jnp.asarray

    def _rec_inputs():
        import jax
        import jax.numpy as jnp
        _gk = jax.random.key(seed)
        x = -0.0003713 + 1 * jax.random.normal(jax.random.fold_in(_gk, 1), (3125, 128), jnp.float32)
        _s = jax.random.randint(jax.random.fold_in(_gk, 2), (50000,), 0, 3125, jnp.int32)
        _d = jax.random.randint(jax.random.fold_in(_gk, 3), (50000,), 0, 3125, jnp.int32)
        _loop = jnp.arange(3125, dtype=jnp.int32)
        src = jnp.concatenate([_s, _d, _loop])
        dst = jnp.concatenate([_d, _s, _loop])
        _o = jnp.argsort(dst, stable=True)
        src = src[_o]
        dst = dst[_o]
        edge_attr_16 = 0.000196303 + 1.00016 * jax.random.normal(jax.random.fold_in(_gk, 11), (103125, 16), jnp.float32)
        edge_type_8 = jax.random.randint(jax.random.fold_in(_gk, 13), (103125,), 0, 8, jnp.int32)
        return (x, src, dst, edge_attr_16, edge_type_8)
    x, src, dst, edge_attr_16, edge_type_8 = _rec_inputs()

    def _L0_gnn_setup():
        import jax, jax.numpy as jnp
        import numpy as np
        N = 3125
        E = 50000
        D_IN = 128
        D_OUT = 128
        key = jax.random.key(seed)
        k1, k2, k3, k4 = jax.random.split(key, 4)
        x = jax.random.normal(k1, (N, D_IN), dtype=jnp.float32)
        edge_index = jax.random.randint(k2, (2, E), 0, N, dtype=jnp.int64)
        scale = 1.0 / np.sqrt(D_IN)
        W = jax.random.uniform(k3, (D_IN, 2 * D_OUT), dtype=jnp.float32, minval=-scale, maxval=scale)
        b = jax.random.uniform(k4, (2 * D_OUT,), dtype=jnp.float32, minval=-scale, maxval=scale)
        return {'x': x, 'edge_index': edge_index, 'W': W, 'b': b}
    _L0_gnn_all = _L0_gnn_setup()
    _L0_gnn_in = {k: v for k, v in _L0_gnn_all.items() if k in ('W', 'b')}
    del _L0_gnn_all

    def _L1_gnn_setup():
        import jax, jax.numpy as jnp
        import numpy as np
        N_NODES = 3125
        WEIGHT = 0.5
        key = jax.random.key(seed)
        k1, k2 = jax.random.split(key)
        x = jax.random.normal(k1, (N_NODES, 128), dtype=jnp.float32)
        edge_index = jax.random.randint(k2, (2, 50000), 0, N_NODES, dtype=jnp.int64)
        return {'x': x, 'edge_index': edge_index}
    _L1_gnn_all = _L1_gnn_setup()
    _L1_gnn_in = {k: v for k, v in _L1_gnn_all.items() if k in ()}
    del _L1_gnn_all

    def _L2_gnn_setup():
        import jax, jax.numpy as jnp
        import numpy as np
        N, E, D_IN, D_OUT, R = (50000, 25000, 128, 128, 8)
        key = jax.random.key(seed)
        ks = jax.random.split(key, 6)
        x = jax.random.normal(ks[0], (N, D_IN), dtype=jnp.float32)
        W_rel = jax.random.normal(ks[1], (R, D_IN, D_OUT), dtype=jnp.float32) * (1.0 / np.sqrt(D_IN))
        W_self_w = jax.random.normal(ks[2], (D_OUT, D_IN), dtype=jnp.float32) * (1.0 / np.sqrt(D_IN))
        W_self_b = jax.random.normal(ks[3], (D_OUT,), dtype=jnp.float32) * 0.01
        edge_index = jax.random.randint(ks[4], (2, E), 0, N, dtype=jnp.int32)
        edge_type = jax.random.randint(ks[5], (E,), 0, R, dtype=jnp.int32)
        return {'x': x, 'W_rel': W_rel, 'W_self_w': W_self_w, 'W_self_b': W_self_b, 'edge_index': edge_index, 'edge_type': edge_type}
    _L2_gnn_all = _L2_gnn_setup()
    _L2_gnn_in = {k: v for k, v in _L2_gnn_all.items() if k in ('W_rel', 'W_self_w', 'W_self_b')}
    del _L2_gnn_all

    def _L3_gnn_setup():
        import jax, jax.numpy as jnp
        import numpy as np
        H, C = (4, 32)
        NEG_SLOPE = 0.2
        LN_EPS = 1e-05
        N_NODES = 50000
        N_EDGES = 50000
        IN_CH = 128
        EDGE_DIM = 16
        key = jax.random.key(seed)
        ks = jax.random.split(key, 10)
        sc = 0.1
        return {'x': jax.random.normal(ks[0], (N_NODES, IN_CH), jnp.float32), 'edge_index': jax.random.randint(ks[1], (2, N_EDGES), 0, N_NODES, jnp.int32), 'edge_attr': jax.random.normal(ks[2], (N_EDGES, EDGE_DIM), jnp.float32), 'W_lin': jax.random.normal(ks[3], (H * C, IN_CH), jnp.float32) * sc, 'W_edge': jax.random.normal(ks[4], (H * C, EDGE_DIM), jnp.float32) * sc, 'att_src': jax.random.normal(ks[5], (1, H, C), jnp.float32) * sc, 'att_dst': jax.random.normal(ks[6], (1, H, C), jnp.float32) * sc, 'att_edge': jax.random.normal(ks[7], (1, H, C), jnp.float32) * sc, 'bias': jnp.zeros((H * C,), jnp.float32), 'ln_gamma': jnp.ones((H * C,), jnp.float32), 'ln_beta': jnp.zeros((H * C,), jnp.float32)}
    _L3_gnn_all = _L3_gnn_setup()
    _L3_gnn_in = {k: v for k, v in _L3_gnn_all.items() if k in ('W_lin', 'W_edge', 'att_src', 'att_dst', 'att_edge', 'bias', 'ln_gamma', 'ln_beta')}
    del _L3_gnn_all
    return {'x': x, 'src': src, 'dst': dst, 'edge_attr_16': edge_attr_16, 'edge_type_8': edge_type_8, 'L0_gnn_W': _L0_gnn_in['W'], 'L0_gnn_b': _L0_gnn_in['b'], 'L2_gnn_W_rel': _L2_gnn_in['W_rel'], 'L2_gnn_W_self_w': _L2_gnn_in['W_self_w'], 'L2_gnn_W_self_b': _L2_gnn_in['W_self_b'], 'L3_gnn_W_lin': _L3_gnn_in['W_lin'], 'L3_gnn_W_edge': _L3_gnn_in['W_edge'], 'L3_gnn_att_src': _L3_gnn_in['att_src'], 'L3_gnn_att_dst': _L3_gnn_in['att_dst'], 'L3_gnn_att_edge': _L3_gnn_in['att_edge'], 'L3_gnn_bias': _L3_gnn_in['bias'], 'L3_gnn_ln_gamma': _L3_gnn_in['ln_gamma'], 'L3_gnn_ln_beta': _L3_gnn_in['ln_beta']}

def reference(x, src, dst, edge_attr_16, edge_type_8, L0_gnn_W, L0_gnn_b, L2_gnn_W_rel, L2_gnn_W_self_w, L2_gnn_W_self_b, L3_gnn_W_lin, L3_gnn_W_edge, L3_gnn_att_src, L3_gnn_att_dst, L3_gnn_att_edge, L3_gnn_bias, L3_gnn_ln_gamma, L3_gnn_ln_beta):
    import jax
    import jax.numpy as jnp

    def _L0_gnn_ref(x, edge_index, W, b):
        import jax, jax.numpy as jnp
        import numpy as np
        N = 3125
        E = 50000
        D_IN = 128
        D_OUT = 128
        n = x.shape[0]
        loops = jnp.arange(n, dtype=edge_index.dtype)
        row = jnp.concatenate([edge_index[0], loops])
        col = jnp.concatenate([edge_index[1], loops])
        deg = jax.ops.segment_sum(jnp.ones_like(col, dtype=x.dtype), col, num_segments=n)
        dinv = jnp.where(deg > 0, jax.lax.rsqrt(deg), 0.0)
        norm = dinv[row] * dinv[col]
        h = x @ W
        msg = h[row] * norm[:, None]
        agg = jax.ops.segment_sum(msg, col, num_segments=n) + b
        a, gate = jnp.split(agg, 2, axis=-1)
        return a * jax.nn.gelu(gate, approximate=False)

    def _L1_gnn_ref(x, edge_index):
        import jax, jax.numpy as jnp
        import numpy as np
        N_NODES = 3125
        WEIGHT = 0.5
        src, dst = (edge_index[0], edge_index[1])
        n = x.shape[0]
        agg_sum = jax.ops.segment_sum(x[src], dst, num_segments=n)
        deg = jax.ops.segment_sum(jnp.ones_like(dst, dtype=x.dtype), dst, num_segments=n)
        agg_mean = agg_sum / jnp.maximum(deg, 1.0)[:, None]
        return x + WEIGHT * agg_mean

    def _L2_gnn_ref(x, W_rel, W_self_w, W_self_b, edge_index, edge_type):
        import jax, jax.numpy as jnp
        import numpy as np
        N, E, D_IN, D_OUT, R = (50000, 25000, 128, 128, 8)
        n = x.shape[0]
        out = x @ W_self_w.T + W_self_b
        src = edge_index[0]
        dst = edge_index[1]
        h = jnp.einsum('nd,rdo->rno', x, W_rel)
        msg = h[edge_type, src]
        agg = jax.ops.segment_sum(msg, dst, num_segments=n)
        deg = jax.ops.segment_sum(jnp.ones_like(dst, dtype=x.dtype), dst, num_segments=n)
        deg = jnp.maximum(deg, 1.0)[:, None]
        out = jax.nn.relu(out + agg / deg)
        return out

    def _L3_gnn_ref(x, edge_index, edge_attr, W_lin, W_edge, att_src, att_dst, att_edge, bias, ln_gamma, ln_beta):
        import jax, jax.numpy as jnp
        import numpy as np
        H, C = (4, 32)
        NEG_SLOPE = 0.2
        LN_EPS = 1e-05
        N_NODES = 50000
        N_EDGES = 50000
        IN_CH = 128
        EDGE_DIM = 16
        N = x.shape[0]
        src, dst = (edge_index[0], edge_index[1])
        xl = (x @ W_lin.T).reshape(N, H, C)
        ef = (edge_attr @ W_edge.T).reshape(-1, H, C)
        x_j = xl[src]
        x_i = xl[dst]
        alpha = (x_i * att_src).sum(-1) + (x_j * att_dst).sum(-1) + (ef * att_edge).sum(-1)
        alpha = jax.nn.leaky_relu(alpha, NEG_SLOPE)
        amax = jax.ops.segment_max(alpha, dst, num_segments=N)
        e = jnp.exp(alpha - amax[dst])
        denom = jax.ops.segment_sum(e, dst, num_segments=N)
        alpha = e / (denom[dst] + 1e-16)
        msg = x_j * alpha[..., None]
        out = jax.ops.segment_sum(msg, dst, num_segments=N)
        out = out.reshape(N, H * C) + bias
        out = out + x
        mu = out.mean(-1, keepdims=True)
        var = ((out - mu) ** 2).mean(-1, keepdims=True)
        out = (out - mu) / jnp.sqrt(var + LN_EPS) * ln_gamma + ln_beta
        return jax.nn.elu(out)
    edge_index = jnp.stack([src, dst])
    h = jnp.maximum(_layernorm(x, axis=-1), 0.0)
    x = x + _L0_gnn_ref(h, edge_index, L0_gnn_W, L0_gnn_b)
    h = jnp.maximum(_layernorm(x, axis=-1), 0.0)
    x = x + _L1_gnn_ref(h, edge_index)
    h = jnp.maximum(_layernorm(x, axis=-1), 0.0)
    x = x + _L2_gnn_ref(h, L2_gnn_W_rel, L2_gnn_W_self_w, L2_gnn_W_self_b, edge_index, edge_type_8)
    h = jnp.maximum(_layernorm(x, axis=-1), 0.0)
    x = x + _L3_gnn_ref(h, edge_index, edge_attr_16, L3_gnn_W_lin, L3_gnn_W_edge, L3_gnn_att_src, L3_gnn_att_dst, L3_gnn_att_edge, L3_gnn_bias, L3_gnn_ln_gamma, L3_gnn_ln_beta)
    return x

_drawn_inputs = setup_inputs


def setup_inputs(seed=0):
    import zlib

    import numpy as np

    out = dict(_drawn_inputs(seed))
    spreads = {'L3_gnn_bias': (0.0, 0.1), 'L3_gnn_ln_gamma': (1.0, 0.2), 'L3_gnn_ln_beta': (0.0, 0.27)}
    factors = {'edge_attr_16': 5.677,
     'L0_gnn_b': 5.839,
     'L2_gnn_W_self_b': 8.0,
     'L3_gnn_W_edge': 6.019,
     'L3_gnn_att_src': 200.0,
     'L3_gnn_att_edge': 5.139,
     'L3_gnn_att_dst': 4.07}
    for name, (base, spread) in spreads.items():
        noise = np.random.default_rng([zlib.crc32(name.encode()), seed]).standard_normal(out[name].shape)
        drawn = base * np.exp(spread * noise) if base else spread * noise
        out[name] = jnp.asarray(drawn.astype(out[name].dtype))
    for name, factor in factors.items():
        out[name] = (out[name] * factor).astype(out[name].dtype)
    return out
```

```python
import concourse.bass as bass
from concourse import mybir
from contextlib import ExitStack

FP = mybir.dt.float32
BF = mybir.dt.bfloat16
F16 = mybir.dt.float16
U8 = mybir.dt.uint8
I32 = mybir.dt.int32
ALU = mybir.AluOpType
ACT = mybir.ActivationFunctionType
AX = mybir.AxisListType
PE = mybir.EngineType.PE
DVE = mybir.EngineType.DVE

P = 128
N = 3125
D = 128
E = 103125
H, C = 4, 32
ED = 16
R = 8
NB = 26
NPAD = NB * P
K = 26
IT = 31
T = K * IT
HK = K // 2
NQ = 7
RG = 4 * K
G = 8
GL = T - (G - 1) * RG
TAIL = E - (T - 1) * P
PAD_NODE = 25 * P - 1
ARENA = 6 * NPAD + 3 * K * ED + 3 * T * H
BIG = 1.0e37
EPS = 1e-5
W_ALL = 16 * 13
OF = {"gcn": 0, "rel": NB, "att": 2 * NB, "end": 3 * NB}
FULL = N // P
REST = N - FULL * P


NP = K // 2
W = 14
HI = 25
BW = HI * P
SLAB = (13 * P, 12 * P)


def mm(n):
    return n * T


class Ring:

    def __init__(self, name, sem, share):
        self.oh = sem(name + "_onehot_ready")
        self.mm = sem(name + "_tile_added")
        self.ix = sem(name + "_index_chunk_copied")
        self.share = share
        self.g = [sem(f"{name}_gathered{k}") for k in range(K // share)]

    def wait_gathered(self, eng, k, m, i):
        if k % self.share == 0:
            eng.wait_ge(self.g[k // self.share], 16 * self.share * (m * IT + i + 1))


def build(nc, x, src, dst, ea, et, w0, b0, wrel, wself, bself, wlin, wedge, attsrc, attdst, attedge,
          bias, gamma, beta, out):
    ctx = ExitStack()
    with ctx:
        def sb(name, shape, dt=FP):
            return ctx.enter_context(nc.sbuf_tensor(name, shape, dt))

        def sem(name):
            return ctx.enter_context(nc.semaphore(name))

        def dram(name, shape, dt=FP):
            return nc.dram_tensor(name, shape, dt, kind="Internal").ap()

        tab = [dram(f"tab{n}", (NPAD, D)) for n in (0, 1)]
        tab2 = dram("tab2", (NPAD * R, D))
        tab3 = dram("tab3", (NPAD, D))
        tabs = [tab[0], tab[1], tab2, tab3]
        block_lin = dram("block_lin", (T,), I32)
        src_lo_row = dram("src_lo_row", (T * P,), BF)
        dst_lo_row = dram("dst_lo_row", (T * P,), BF)
        ends = dram("ends", (5, H, T))
        carries = dram("carries", (2, H, T))

        X = sb("X", [P, NB, D])
        Hn = sb("Hn", [P, NB, D])
        arena = sb("arena", [P, ARENA])
        at = 0

        def carve(n):
            nonlocal at
            at += n
            assert at <= ARENA
            return arena[:, at - n:at]
        agg = carve(NPAD).rearrange("p (b d) -> p b d", d=D)
        cen = carve(NPAD).rearrange("p (b d) -> p b d", d=D)
        oh = carve(K * 256).rearrange("p (k w) -> p k w", w=256)
        xg = carve(K * D).rearrange("p (k d) -> p k d", d=D)
        xw = carve(K * D).rearrange("p (k d) -> p k d", d=D)
        ea_buf = carve(2 * K * ED).rearrange("p (s k f) -> p s k f", s=2, f=ED)
        ea_tmp = carve(K * ED).rearrange("p (k f) -> p k f", f=ED)
        EA = carve(T * H).rearrange("p (i h k) -> p i h k", h=H, k=K)
        SDZM = carve(2 * T * H)
        count = arena[:, ARENA - HI * BW // 4:ARENA].bitcast(U8).rearrange("p (b d) -> p b d", d=BW)
        parts = arena[:, NPAD:NPAD + 3 * NPAD // 2].bitcast(BF).rearrange("p (n d) -> p n d", n=3)
        left = arena[:, NPAD + 3 * NPAD // 2:3 * NPAD]
        slabs = [left[:, n * (NPAD // 4):n * (NPAD // 4) + SLAB[n] // 2].bitcast(BF) for n in range(2)]
        src_oh = arena[:, 2 * NPAD:2 * NPAD + K * P // 2].bitcast(BF).rearrange("p (k n) -> p k n", k=K)
        pair_at = (0, 2 * NPAD + K * P // 2)
        assert pair_at[1] + NP * HI * W // 2 <= ARENA - HI * BW // 4
        pair_oh = [arena[:, a:a + NP * HI * W // 2].bitcast(BF).rearrange("p (s n) -> p s n", s=NP) for a in pair_at]
        sq = oh.rearrange("p k w -> p (k w)")[:, 0:NPAD].rearrange("p (b d) -> p b d", d=D)
        t2_stage = xg.rearrange("p k d -> p (k d)")[:, 0:2 * R * D].rearrange("p (s n) -> p s n", s=2)
        at = 0
        SROW = IT * P
        zt = carve(SROW)
        brk = carve(SROW)
        dt_ = carve(SROW)
        fw = carve(SROW)
        bw = carve(SROW)
        ch = arena[0:H, 0:9 * T].rearrange("h (q t) -> h q t", t=T)
        at = NPAD
        rows = carve(4 * K * P // 2).bitcast(BF).rearrange("p (w s n) -> p w s n", w=2, s=2)
        ohs = carve(NQ * 2 * P).bitcast(BF).rearrange("p (s n) -> p s n", s=NQ)
        ohd = carve(NQ * 2 * P).bitcast(BF).rearrange("p (s n) -> p s n", s=NQ)
        hi_mask = carve(2 * K * NB).rearrange("p (s k b) -> p s k b", s=2, b=NB)
        prod = carve(2 * 4 * NB * H).rearrange("p (s n) -> p s n", s=2)
        sd_two = carve(2 * K * 2 * H).rearrange("p (s k w) -> p s k w", s=2, w=2 * H)
        at = NPAD * 2
        rows_i = [carve(G * P).bitcast(I32).rearrange("p (g e) -> p g e", e=P) for _ in range(3)]
        rows_f = [carve(G * P).rearrange("p (g e) -> p g e", e=P) for _ in range(5)]
        lo_i = carve(G * P).bitcast(I32).rearrange("p (g e) -> p g e", e=P)
        lo_b = [carve(G * P // 2).bitcast(BF).rearrange("p (g e) -> p g e", e=P) for _ in range(2)]

        rel = sb("rel", [P, T])
        hi = sb("hi", [P, T])
        idx = sb("idx", [P, T], I32)
        hidx = sb("hidx", [P, T], I32)
        idx_buf = sb("idx_buf", [P, K], I32)
        SD, ZM = (SDZM[:, n * T * H:(n + 1) * T * H].rearrange("p (i h k) -> p i h k", h=H, k=K) for n in range(2))
        code = sb("code", [P, T])
        slo = sb("slo", [P, T])
        base_row = sb("base_row", [1, T // 2], I32)
        base_f = sb("base_f", [1, T // 2])
        io_c = sb("io_c", [P, HI * W], I32)
        wide_c = sb("wide_c", [P, HI * W], F16)
        total = sb("total", [P, 1])
        flag = sb("flag", [1, 1], I32)
        ones_b = sb("ones_b", [P, 1], BF)
        inside = agg.rearrange("p b d -> p (b d)")[:, 0:T]
        in_tmp = agg.rearrange("p b d -> p (b d)")[:, T:2 * T]
        b0_lin = sb("b0_lin", [RG, G], I32)
        b0_f = sb("b0_f", [RG, G])
        b0_row = sb("b0_row", [1, IT, 28], I32)

        io_p = sb("io_p", [P, 1], I32)
        io_w = sb("io_w", [P, 256], I32)
        part = sb("part", [P, 1])
        wide = sb("wide", [P, 256])
        wide_b = sb("wide_b", [P, 256], BF)
        ident = sb("ident", [P, P])
        ones = sb("ones", [P, P])
        zeros = sb("zeros", [P, 512], BF)
        zero_w = sb("zero_w", [P, P], BF)
        deg = sb("deg", [P, NB])
        dinv = sb("dinv", [P, NB])
        rdeg = sb("rdeg", [P, NB])
        st = sb("st", [P, 6, NB])
        stage = sb("stage", [P, 2, P])
        lt = sb("lt", [P, 2, P])
        ab = sb("ab", [P, 2, P])
        gl = sb("gl", [P, 2, P])
        W0 = sb("W0", [P, 2 * D])
        B0 = sb("B0", [1, 2 * D])
        WR = sb("WR", [P, R, D])
        WSn = sb("WSn", [P, D])
        WS = sb("WS", [P, D])
        BS = sb("BS", [1, D])
        WLn = sb("WLn", [P, D])
        WL = sb("WL", [P, D + 2 * H])
        WE = sb("WE", [P, ED])
        att = sb("att", [P, 3])
        head = sb("head", [P, H])
        att3 = sb("att3", [P, 3, H])
        att_wide = sb("att_wide", [P, H, P])
        U = sb("U", [P, H, ED])
        vecs = sb("vecs", [P, 3, D])
        ssrc = sb("ssrc", [P, NB, H])
        sdst = sb("sdst", [P, NB + 1, H])
        den = sb("den", [P, NB, H])
        ssrc3 = sb("ssrc3", [P, 3, NB * H], BF)
        sdst3 = sb("sdst3", [P, 3, (NB + 1) * H], BF)
        split_tmp = sb("split_tmp", [P, (NB + 1) * H])
        ends_sb = sb("ends_sb", [RG, 5, IT])
        ends_t = sb("ends_t", [IT, 5, RG])
        car_t = sb("car_t", [IT, 2, RG])
        car_in = sb("car_in", [RG, 2, IT])
        rden = sb("rden", [P, NB, H])
        in_block = sb("in_block", [P, 2, 2, K])
        e_buf = sb("e_buf", [P, 2, HK, H])
        e3_buf = sb("e3_buf", [P, 2, HK, 3 * H], BF)
        E3 = SDZM[:, 0:3 * T * H // 2].bitcast(BF).rearrange("p (n t) -> p n t", n=3)
        oh_b = agg.rearrange("p b d -> p (b d)").bitcast(BF).rearrange("p (k w) -> p k w", w=2 * P)

        ps = ctx.enter_context(nc.psum_tensor("ps", [P, 4096], FP))
        BK = 512
        acc = ps[:, 0:7 * BK]
        small = ps[:, 7 * BK:8 * BK]
        turned = [ps[:, (6 + s) * BK:(6 + s) * BK + P] for s in range(2)]

        s_rows = sem("index_rows_loaded")
        s_x = sem("x_loaded")
        s_w = sem("weights_loaded")
        s_io = sem("iotas_written")
        s_v = sem("vector_steps")
        s_a = sem("scalar_steps")
        s_t = sem("index_turned")
        s_tc = sem("index_copied")
        s_scr = sem("index_scratch_written")
        s_b0 = sem("block_row_loaded")
        s_pe0 = sem("weights_turned")
        slow, main = Ring("slow", sem, HK), Ring("main", sem, 1)
        s_z = sem("psum_zeroed")
        s_acc_free = sem("psum_read")
        s_tabw = sem("table_written")
        s_tabr = sem("table_ready")
        s_ea = [sem(f"edge_attr_loaded{k}") for k in range(2)]
        s_eau = sem("edge_attr_used")
        s_xw = sem("rows_weighted")
        s_st = sem("block_staged")
        s_tp = sem("block_turned")
        s_lt = sem("turned_copied")
        s_mo = sem("block_multiplied")
        s_of = sem("block_taken")
        s_ae = sem("act_block_out")
        s_t2 = [sem(f"tab2_block_written{k}") for k in range(2)]
        s_row = [sem(f"lo_rows_loaded{k}") for k in range(2)]
        s_rowu = sem("lo_rows_used")
        s_qoh = sem("quad_onehots")
        s_qmm = sem("quad_picked")
        s_qd = sem("quad_reduced")
        s_pass_a = sem("pass_a_done")
        s_zs = sem("scores_staged")
        s_zt = sem("scores_turned")
        s_ztc = sem("scores_turned_copied")
        s_dt = sem("dst_rows_loaded")
        s_ends = sem("ends_moved")
        s_out = sem("out_written")
        s_et = sem("edge_term_steps")
        s_ae0 = sem("gelu_block")
        s_xb = sem("block_added")
        s_hm = sem("hi_mask_written")
        s_pr = sem("quad_steps")
        s_qd = sem("quad_psum_read")
        s_eb = sem("weights_staged")
        s_base = sem("pair_bases_loaded")
        s_bc = sem("pair_bases_spread")
        s_cnt0 = sem("counts_zeroed")
        s_po = sem("pair_onehots")
        s_pm = sem("pair_multiplied")
        s_pa = sem("pair_added")
        s_sl = [sem(f"slab_ready{n}") for n in range(2)]
        s_su = [sem(f"slab_used{n}") for n in range(2)]
        s_tot = sem("total_summed")
        s_flag = sem("flag_written")
        s_sv = sem("vector_steps_slow")
        s_dense = sem("dense_sums_done")
        s_split = [sem(f"table_split{n}") for n in range(2)]
        s_tabs = sem("slow_table_ready")
        s_prod = sem("quad_masked")
        s_sdc = sem("two_blocks_read")
        s_rq = sem("reduced")
        s_ect = sem("ends_turned")
        s_held = sem("pool_waits_over")
        zmf = ZM[:, :, :, :].rearrange("p i h k -> p (i h k)")
        eaf = EA[:, :, :, :].rearrange("p i h k -> p (i h k)")
        ready = {m: sem("ready_" + m) for m in (
            "pads_set index_rows index_cols att weights c0 c0_var ln0_sq ln0_std deg sqrt_deg table0 agg0 "
            "c1 c1_var ln1_sq ln1_std table1 c2 c2_var ln2_sq ln2_std h2 c3 c3_var ln3_sq ln3_std h3 table3 "
            "dst_pads ends_cols ends carries carries_read alpha exp c4 c4_var ln4_sq ln4_std elu_min elu_exp "
            "score_tables weights3 bases counted totals parts0 parts1 final").split()}

        block = ctx.enter_context(nc.Block())

        class Steps:

            def __init__(self, eng, s):
                self.eng, self.sem, self.n = eng, s, 0

            def __call__(self, ins):
                ins.then_inc(self.sem, 1)
                self.n += 1
                self.eng.wait_ge(self.sem, self.n)

        def take_flag(eng):
            eng.wait_ge(s_flag, 1)
            return eng.value_load(flag[0:1, 0:1], min_val=0, max_val=1)

        @block.sync
        def _(sp):
            sp.wait_ge(ready["pads_set"], 1)
            for n, a in enumerate((dst, src, et)):
                full = (G - 1) * RG * P
                sp.dma_start(rows_i[n][0:RG, 0:G - 1, :],
                             a[0:full].rearrange("(g p e) -> p g e", p=RG, e=P)).then_inc(s_rows, 16)
                last = full + (GL - 1) * P
                sp.dma_start(rows_i[n][0:GL - 1, G - 1, :],
                             a[full:last].rearrange("(p e) -> p e", e=P)).then_inc(s_rows, 16)
                sp.dma_start(rows_i[n][GL - 1:GL, G - 1, 0:TAIL],
                             a[last:E].rearrange("(p e) -> p e", p=1)).then_inc(s_rows, 16)
            sp.dma_start(X[:, 0:FULL, :], x[0:FULL * P, :].rearrange("(b p) d -> p b d", p=P)).then_inc(s_x, 16)
            sp.dma_start(X[0:REST, FULL, :], x[FULL * P:N, :]).then_inc(s_x, 16)
            loads = [
                (W0[:, :], w0), (B0[:, :], b0.rearrange("(p d) -> p d", p=1)),
                (WR[:, :, :], wrel.rearrange("r k d -> k r d")),
                (WSn[:, :], wself), (BS[:, :], bself.rearrange("(p d) -> p d", p=1)),
                (WLn[:, :], wlin), (WE[:, :], wedge),
            ]
            loads += [(att[:, n:n + 1], a[0, :, :].rearrange("h (c o) -> (h c) o", o=1))
                      for n, a in enumerate((attsrc, attdst, attedge))]
            loads += [(vecs[:, n, :], a.rearrange("(p d) -> p d", p=1).broadcast_to([P, D]))
                      for n, a in enumerate((bias, gamma, beta))]
            for o, i in loads:
                sp.dma_start(o, i).then_inc(s_w, 16)
            assert 16 * len(loads) == W_ALL
            sp.dma_start(base_row[0:1, 0:T // 2 - 1].unsqueeze(2),
                         dst[0:(T - 2) * P].rearrange("(o n e) -> o n e", o=1, e=2 * P)[:, :, 0:1],
                         allow_slow_non_contiguous=True).then_inc(s_base, 16)
            sp.dma_start(base_row[0:1, T // 2 - 1:T // 2],
                         dst[(T - 2) * P:(T - 2) * P + 1].rearrange("(o k) -> o k", o=1)).then_inc(s_base, 16)

            sp.wait_ge(ready["index_rows"], 1)
            for g in range(G):
                n = RG if g < G - 1 else GL
                sp.dma_start(block_lin[g * RG:g * RG + n].rearrange("(p o) -> p o", o=1),
                             b0_lin[0:n, g:g + 1]).then_inc(s_scr, 16)
            for row, b in ((src_lo_row, lo_b[0]), (dst_lo_row, lo_b[1])):
                sp.dma_start(row[0:(G - 1) * RG * P].rearrange("(g p e) -> p g e", p=RG, e=P),
                             b[0:RG, 0:G - 1, :]).then_inc(s_scr, 16)
                sp.dma_start(row[(G - 1) * RG * P:T * P].rearrange("(p e) -> p e", e=P),
                             b[0:GL, G - 1, :]).then_inc(s_scr, 16)
            sp.wait_ge(s_scr, 16 * (G + 4))
            sp.wait_ge(ready["pads_set"], 1)
            sp.dma_start(b0_row[0:1, :, 0:K], block_lin.rearrange("(o i k) -> o i k", o=1, k=K)).then_inc(s_b0, 16)

            def write_table(n, mark):
                sp.wait_ge(ready[mark], 1)
                sp.dma_start(tabs[n].rearrange("(b p) d -> p b d", p=P), agg[:, :, :]).then_inc(s_tabr, 16)

            def slow_table(n, mark):
                sp.wait_ge(ready[mark], 1)
                sp.dma_start(tabs[n].rearrange("(b p) d -> p b d", p=P), agg[:, :, :]).then_inc(s_tabs, 16)

            fits = take_flag(sp)
            with sp.If(fits == 0):
                slow_table(0, "table0")
                slow_table(1, "table1")

            t2 = tab2.rearrange("(b p r) d -> b p (r d)", p=P, r=R)
            with sp.Fori(0, NB // 2) as i:
                for s in range(2):
                    sp.wait_ge(s_of, OF["rel"] + 2 * i + s + 3)
                    sp.dma_start(t2[bass.ds(2 * i + s, 1), :, :].rearrange("o p n -> (o p) n"), t2_stage[:, s, :]).then_inc(s_t2[s], 16)
            def edge_chunk(i, s, tiles):
                sp.dma_start(ea_buf[:, s, 0:tiles, :],
                             ea[bass.ds(i * (K * P), tiles * P), :].rearrange("(k p) f -> p k f", p=P)
                             ).then_inc(s_ea[s], 16)
            with sp.Fori(0, IT // 2) as j:
                for s in range(2):
                    sp.wait_ge(s_eau, 2 * j + s + 1)
                    edge_chunk(2 * j + s, s, K)
            sp.wait_ge(s_eau, IT)
            edge_chunk(IT - 1, 0, K - 1)
            sp.dma_start(ea_buf[0:TAIL, 0, K - 1, :], ea[(T - 1) * P:E, :]).then_inc(s_ea[0], 16)

            write_table(3, "table3")

            def lo_rows(i, s):
                for w, row in enumerate((src_lo_row, dst_lo_row)):
                    sp.dma_start(rows[:, w, s, :], row[bass.ds(i * (K * P), K * P)]
                                 .rearrange("(o n) -> o n", o=1).broadcast_to([P, K * P])).then_inc(s_row[s], 16)
            sp.wait_ge(ready["table3"], 1)
            with sp.Fori(0, IT // 2) as j:
                for s in range(2):
                    sp.wait_ge(s_rowu, 2 * j + s + 1)
                    lo_rows(2 * j + s, s)
            sp.wait_ge(s_rowu, IT)
            lo_rows(IT - 1, 0)

            sp.wait_ge(ready["dst_pads"], 1)
            for h in range(H):
                full = (IT - 1) * K * P
                sp.dma_start(dt_[h * K:(h + 1) * K, 0:(IT - 1) * P].bitcast(I32).rearrange("k (i e) -> k i e", e=P),
                             dst[0:full].rearrange("(i k e) -> k i e", k=K, e=P)).then_inc(s_dt, 16)
                sp.dma_start(dt_[h * K:h * K + K - 1, (IT - 1) * P:IT * P].bitcast(I32),
                             dst[full:full + (K - 1) * P].rearrange("(k e) -> k e", e=P)).then_inc(s_dt, 16)
                sp.dma_start(dt_[h * K + K - 1:(h + 1) * K, (IT - 1) * P:(IT - 1) * P + TAIL].bitcast(I32),
                             dst[full + (K - 1) * P:E].rearrange("(k e) -> k e", k=1)).then_inc(s_dt, 16)
            sp.wait_ge(ready["ends"], 1)
            for q in range(5):
                sp.dma_start(ends[q, :, :].rearrange("h (i k) -> i h k", k=K),
                             ends_t[:, q, :].rearrange("i (h k) -> i h k", k=K)).then_inc(s_ends, 16)
            sp.wait_ge(s_ends, 16 * 5)
            sp.dma_start(ch[:, 0:5, :], ends.rearrange("q h t -> h q t")).then_inc(s_ends, 16)
            sp.wait_ge(ready["carries"], 1)
            sp.dma_start(carries.rearrange("q h t -> h q t"), ch[:, 7:9, :]).then_inc(s_ends, 16)
            sp.wait_ge(s_ends, 16 * 7)
            for q in range(2):
                sp.dma_start(car_t[:, q, :].rearrange("i (h k) -> i h k", k=K),
                             carries[q, :, :].rearrange("h (i k) -> i h k", k=K)).then_inc(s_ends, 16)

            sp.wait_ge(ready["final"], 1)
            sp.dma_start(out[0:FULL * P, :].rearrange("(b p) d -> p b d", p=P), X[:, 0:FULL, :]).then_inc(s_out, 16)
            sp.dma_start(out[FULL * P:N, :], X[0:REST, FULL, :]).then_inc(s_out, 16)
            sp.wait_ge(s_out, 32)

        @block.gpsimd
        def _(pool):
            pool.iota(io_p[:, :], [[0, 1]], base=0, channel_multiplier=1).then_inc(s_io, 1)
            pool.iota(io_w[:, :], [[1, 256]], base=0, channel_multiplier=0).then_inc(s_io, 1)
            pool.memset(ones[:, :], 1.0).then_inc(s_io, 1)
            pool.memset(zeros[:, :], 0.0).then_inc(s_io, 1)
            pool.memset(zero_w[:, :], 0.0).then_inc(s_io, 1)
            pool.iota(io_c[:, :], [[1, HI * W]], base=0, channel_multiplier=0).then_inc(s_io, 1)
            pool.memset(ones_b[:, :], 1.0).then_inc(s_io, 1)
            pool.wait_ge(ready["index_cols"], 1)
            pool.wait_ge(s_scr, 16 * (G + 4))
            pool.memset(count.rearrange("p b d -> p (b d)").bitcast(I32), 0).then_inc(s_cnt0, 1)

            def gather(r, n, m, table, indices):
                with pool.Fori(0, IT) as i:
                    for half in range(2):
                        pool.wait_ge(r.mm, mm(n) + i * K + HK * (half + 1))
                        pool.sem_inc(s_held, 1)
                        pool.tensor_copy(idx_buf[:, half * HK:(half + 1) * HK],
                                         indices[:, bass.ds(i * K + half * HK, HK)]).then_inc(r.ix, 1)
                        pool.wait_ge(r.ix, 2 * IT * m + 2 * i + half + 1)
                        pool.sem_inc(s_held, 1)
                        for k in range(half * HK, (half + 1) * HK):
                            pool.indirect_dma_start(
                                out=xg[:, k, :], out_offset=None, in_=table,
                                in_offset=bass.IndirectOffsetOnAxis(ap=idx_buf[:, k:k + 1], axis=0)
                            ).then_inc(r.g[k // r.share], 16)

            fits = take_flag(pool)
            with pool.If(fits == 0):
                for n in range(2):
                    pool.wait_ge(s_tabs, 16 * (n + 1))
                    gather(slow, n + 1, n, tabs[n], idx)
            for t in s_t2:
                pool.wait_ge(t, 16 * (NB // 2))
            gather(main, 0, 0, tab2, hidx)
            pool.wait_ge(s_tabr, 16)
            pool.wait_ge(ready["alpha"], 1)
            gather(main, 1, 1, tab3, idx)

        @block.scalar
        def _(act):
            step = Steps(act, s_a)

            def mark(name):
                act.sem_inc(ready[name], 1)

            def std(v_mark, name):
                act.wait_ge(ready[v_mark], 1)
                step(act.activation(sq, cen, ACT.Square))
                mark(name + "_sq")
                act.wait_ge(ready[v_mark + "_var"], 1)
                step(act.activation(st[:, 3, :], st[:, 2, :], ACT.Sqrt))
                mark(name + "_std")

            def turn_blocks(n, source, mark_v, mm_used):
                act.wait_ge(ready[mark_v], 1)
                def pair(i, first=False):
                    for s in range(2):
                        act.activation(stage[:, s, :], source[:, bass.ds(2 * i + s, 1), :].rearrange("p o d -> p (o d)"), ACT.Copy).then_inc(s_st, 1)
                    for s in range(2):
                        act.wait_ge(s_tp, NB * n + 2 * i + s + 1)
                        act.wait_ge(s_of, mm_used + 2 * i + s + 1)
                        act.activation(lt[:, s, :], turned[s], ACT.Copy).then_inc(s_lt, 1)
                    if n == 0:
                        for s in range(2):
                            act.wait_ge(s_mo, 2 * i + s + 1)
                            act.activation(gl[:, s, :], ps[:, s * BK + D:s * BK + 2 * D], ACT.Gelu).then_inc(s_ae0, 1)
                    if n == 1:
                        for s in range(2):
                            act.wait_ge(s_mo, NB + 2 * i + s + 1)
                            if not first:
                                act.wait_ge(s_t2[s], 16 * i)
                            act.activation(t2_stage[:, s, 512:1024],
                                           ps[:, (3 * s + 1) * BK:(3 * s + 2) * BK], ACT.Copy).then_inc(s_ae, 1)
                pair(0, True)
                with act.Fori(1, NB // 2) as i:
                    pair(i)

            act.sem_inc(s_ztc, 2)
            def cast_slabs(n):
                with act.Fori(0, HI) as b:
                    act.wait_ge(s_su[0], n * HI + b + 1)
                    act.activation(slabs[0], count[:, bass.ds(b, 1), 0:SLAB[0]].rearrange("p o d -> p (o d)"),
                                   ACT.Copy).then_inc(s_sl[0], 1)

            std("c0", "ln0")
            act.wait_ge(ready["counted"], 1)
            cast_slabs(0)
            act.wait_ge(ready["deg"], 1)
            step(act.activation(dinv[:, :], st[:, 4, :], ACT.Sqrt))
            mark("sqrt_deg")
            fits = take_flag(act)
            with act.If(fits > 0):
                act.wait_ge(ready["parts0"], 1)
                cast_slabs(1)
            turn_blocks(0, agg, "agg0", OF["gcn"])
            std("c1", "ln1")
            with act.If(fits > 0):
                act.wait_ge(ready["parts1"], 1)
                cast_slabs(2)
            std("c2", "ln2")
            turn_blocks(1, Hn, "h2", OF["rel"])
            std("c3", "ln3")
            turn_blocks(2, Hn, "h3", OF["att"])
            def out_z(i, s):
                act.wait_ge(s_zt, i + 1)
                act.activation(zt[0:RG, bass.ds(i * P, P)], ps[0:RG, s * BK:s * BK + P], ACT.Copy).then_inc(s_ztc, 1)

            def out_m(i, s):
                act.wait_ge(s_zt, IT + i + 1)
                act.activation(ZM[:, bass.ds(i, 1), :, :].rearrange("p o h k -> p (o h k)"),
                               ps[:, s * BK:s * BK + RG], ACT.Copy).then_inc(s_ztc, 1)
            for f in (out_z, out_m):
                with act.Fori(0, IT // 2) as j:
                    for s in range(2):
                        f(2 * j + s, s)
                f(IT - 1, 0)
            act.wait_ge(ready["alpha"], 1)
            step(act.activation(EA[:, :, :, :], EA[:, :, :, :], ACT.Exp))
            mark("exp")
            act.wait_ge(ready["weights3"], 1)
            with act.Fori(0, IT) as i:
                for half in range(2):
                    act.wait_ge(main.mm, mm(1) + i * K + HK * (half + 1))
                    act.activation(e_buf[:, half, :, :], EA[:, bass.ds(i, 1), :, half * HK:(half + 1) * HK]
                                   .rearrange("p o h k -> p (o k) h"), ACT.Copy)
                    for n in range(3):
                        last = act.activation(e3_buf[:, half, :, n * H:(n + 1) * H],
                                              E3[:, n, bass.ds(i * (H * K), H * K)].rearrange("p (h k) -> p k h", h=H)
                                              [:, half * HK:(half + 1) * HK, :], ACT.Copy)
                    last.then_inc(s_eb, 1)
            std("c4", "ln4")
            act.wait_ge(ready["elu_min"], 1)
            step(act.activation(sq, agg, ACT.Exp))
            mark("elu_exp")

        @block.vector
        def _(dve):
            step = Steps(dve, s_v)

            def mark(name):
                dve.sem_inc(ready[name], 1)

            def tt(o, a, b, op):
                step(dve.tensor_tensor(o, a, b, op))

            def ts(o, a, s1, s2, op0, op1=None):
                if op1 is None:
                    step(dve.tensor_scalar(o, a, s1, None, op0))
                else:
                    step(dve.tensor_scalar(o, a, s1, s2, op0, op1))

            def split3(parts, a, left):
                for n in range(3):
                    source = a if n == 0 else left
                    step(dve.tensor_copy(parts[:, n, :], source))
                    if n < 2:
                        tt(left, source, parts[:, n, :], ALU.subtract)

            def across(ap, n=D):
                return ap.unsqueeze(2).broadcast_to([ap.shape[0], ap.shape[1], n])

            def layernorm(name, mark_c):
                source = X if name != "ln4" else agg
                step(dve.tensor_reduce(st[:, 0, :], source[:, :, :], AX.X, ALU.add))
                ts(st[:, 1, :], st[:, 0, :], 1.0 / D, None, ALU.mult)
                tt(cen, source[:, :, :], across(st[:, 1, :]), ALU.subtract)
                mark(mark_c)
                dve.wait_ge(ready[name + "_sq"], 1)
                step(dve.tensor_reduce(st[:, 0, :], sq, AX.X, ALU.add))
                ts(st[:, 2, :], st[:, 0, :], 1.0 / D, EPS, ALU.mult, ALU.add)
                mark(mark_c + "_var")
                dve.wait_ge(ready[name + "_std"], 1)
                step(dve.reciprocal(st[:, 5, :], st[:, 3, :]))
                tt(cen, cen, across(st[:, 5, :]), ALU.mult)

            dve.sem_inc(s_of, 2)
            dve.sem_inc(s_qd, 7)
            dve.sem_inc(s_pa, NP)
            dve.sem_inc(s_eau, 2)
            dve.sem_inc(s_rowu, 2)

            for n in range(3):
                step(dve.memset(rows_i[n][:, :, :], 0 if n == 2 else PAD_NODE))
            step(dve.memset(X[:, :, :], 0.0))
            step(dve.memset(b0_row[:, :, :], 0))
            mark("pads_set")
            step(dve.memset(head[:, :], 0.0))
            for h in range(H):
                step(dve.memset(head[h * C:(h + 1) * C, h:h + 1], 1.0))
            step(dve.memset(sdst[:, :, :], 0.0))
            dve.wait_ge(s_io, 7)
            step(dve.tensor_copy(wide_c[:, :], io_c[:, :]))
            step(dve.tensor_copy(part[:, :], io_p[:, :]))
            step(dve.tensor_copy(wide[:, :], io_w[:, :]))
            step(dve.tensor_copy(wide_b[:, :], io_w[:, :]))
            ts(ident[:, :], wide[:, 0:P], part[:, 0:1], None, ALU.is_equal)
            dve.wait_ge(s_rows, 16 * 9)
            di, si, ti = (r[0:RG, :, :] for r in rows_i)
            relf, srcf, hidf, hif, dstf = (r[0:RG, :, :] for r in rows_f)
            step(dve.tensor_single_scalar(b0_lin[:, :].unsqueeze(2), di[:, :, 0:1], 7, ALU.arith_shift_right))
            step(dve.tensor_copy(b0_f[:, :], b0_lin[:, :]))
            ts(b0_f[:, :], b0_f[:, :], float(P), None, ALU.mult)
            step(dve.tensor_copy(relf, di))
            step(dve.tensor_copy(dstf, di))
            tt(relf, relf, across(b0_f[:, :], P), ALU.subtract)
            step(dve.tensor_copy(srcf, si))
            step(dve.tensor_copy(hidf, ti))
            step(dve.scalar_tensor_tensor(hidf, srcf, float(R), hidf, ALU.mult, ALU.add))
            step(dve.tensor_single_scalar(lo_i[0:RG, :, :], si, P - 1, ALU.bitwise_and))
            step(dve.tensor_copy(lo_b[0][0:RG, :, :], lo_i[0:RG, :, :]))
            step(dve.tensor_copy(hif, lo_i[0:RG, :, :]))
            tt(hif, srcf, hif, ALU.subtract)
            ts(hif, hif, 1.0 / P, None, ALU.mult)
            step(dve.tensor_single_scalar(lo_i[0:RG, :, :], di, P - 1, ALU.bitwise_and))
            step(dve.tensor_copy(lo_b[1][0:RG, :, :], lo_i[0:RG, :, :]))
            mark("index_rows")
            for n, o in enumerate((rel, idx, hidx, hi, code)):
                for g in range(G):
                    m = RG if g < G - 1 else GL
                    c = n * G + g
                    dve.wait_ge(s_t, c + 1)
                    dve.tensor_copy(o[:, g * RG:g * RG + m], ps[:, (c % 8) * BK:(c % 8) * BK + m]).then_inc(s_tc, 1)
            dve.wait_ge(s_tc, 5 * G)
            step(dve.scalar_tensor_tensor(slo[:, :], hi[:, :], -float(P), idx[:, :], ALU.mult, ALU.add))
            dve.wait_ge(s_base, 32)
            step(dve.tensor_copy(base_f[:, :], base_row[:, :]))
            mark("bases")
            dve.wait_ge(s_bc, 1)
            c3 = code[:, :].rearrange("p (n w) -> p n w", w=2)
            tt(c3, c3, across(ps[:, 0:T // 2], 2), ALU.subtract)
            ts(inside[:, :], code[:, :], 0.0, None, ALU.is_ge)
            ts(in_tmp, code[:, :], float(W), None, ALU.is_lt)
            tt(inside[:, :], inside[:, :], in_tmp, ALU.mult)
            step(dve.scalar_tensor_tensor(code[:, :], hi[:, :], float(W), code[:, :], ALU.mult, ALU.add))
            step(dve.scalar_tensor_tensor(code[:, :], code[:, :], 1.0, inside[:, :], ALU.add, ALU.mult))
            ts(code[:, :], code[:, :], 1.0, None, ALU.subtract)
            mark("index_cols")
            dve.wait_ge(s_scr, 16 * (G + 4))

            dve.wait_ge(s_w, W_ALL)
            for n in range(3):
                ts(att3[:, n, :], head[:, :], att[:, n:n + 1], None, ALU.mult)
            for h in range(H):
                ts(att_wide[:, h, :], ones[:, :], att3[:, 2, h:h + 1], None, ALU.mult)
            mark("att")
            dve.wait_ge(s_pe0, 1)
            step(dve.tensor_copy(WS[:, :], ps[:, 0:D]))
            step(dve.tensor_copy(WL[:, 0:D], ps[:, BK:BK + D]))
            step(dve.tensor_copy(WL[:, D:D + 2 * H], ps[:, 2 * BK:2 * BK + 2 * H]))
            step(dve.tensor_copy(U[:, :, :], ps[:, 3 * BK:3 * BK + H * ED].rearrange("p (h f) -> p h f", f=ED)))
            mark("weights")

            dve.wait_ge(s_x, 32)
            layernorm("ln0", "c0")
            ts(cen, cen, 0.0, None, ALU.max)

            def onehots(r, n, i, k):
                if k % HK == 0:
                    dve.wait_ge(r.mm, mm(n) + i * K + k + HK)
                dve.tensor_scalar(oh[:, k, :], wide[:, :], rel[:, bass.ds(i * K + k, 1)], None,
                                  ALU.is_equal).then_inc(r.oh, 1)

            def load_bases(i, p):
                n = min(4, NP - p)
                return nc.values_load_multi_w_load_instructions(
                    base_row[0:1, bass.ds(i * NP + p, n)],
                    engines=(DVE,), min_val=0, max_val=N - 1,
                    skip_runtime_bounds_check_because="destinations are nodes")[1]

            def pair_onehots(i, p):
                dve.wait_ge(s_pm, NP * i + p + 1)
                for k in (2 * p, 2 * p + 1):
                    dve.tensor_scalar(src_oh[:, k, :], wide_b[:, 0:P], slo[:, bass.ds(i * K + k, 1)], None, ALU.is_equal)
                    last = dve.tensor_scalar(pair_oh[k % 2][:, p, :], wide_c[:, :], code[:, bass.ds(i * K + k, 1)], None,
                                             ALU.is_equal)
                last.then_inc(s_po, 1)

            def add_pair(i, p, regs):
                dve.wait_ge(s_pm, NP * i + p + 1 + NP)
                dve.wait_ge(s_pa, NP * i + p + NP)
                window = count[:, :, bass.ds(regs[p % 4], W)]
                dve.tensor_tensor(window, window, ps[:, (p % 8) * BK:(p % 8) * BK + HI * W].rearrange("p (b w) -> p b w", w=W),
                                  ALU.add).then_inc(s_pa, 1)

            dve.wait_ge(s_cnt0, 1)
            with dve.Fori(0, IT) as i:
                for p in range(NP + 2):
                    if p < NP:
                        pair_onehots(i, p)
                    if p >= 2:
                        if (p - 2) % 4 == 0:
                            regs = load_bases(i, p - 2)
                        add_pair(i, p - 2, regs)
            dve.wait_ge(s_pa, NP + T // 2)
            mark("counted")

            def cast_slabs(n, done):
                with dve.Fori(0, HI) as b:
                    dve.wait_ge(s_su[1], n * HI + b + 1)
                    dve.tensor_copy(slabs[1], count[:, bass.ds(b, 1), SLAB[0]:BW].rearrange("p o d -> p (o d)")
                                    ).then_inc(s_sl[1], 1)
                dve.wait_ge(s_dense, done)

            cast_slabs(0, 1)
            step(dve.tensor_copy(deg[:, :], small[:, 0:NB]))
            step(dve.tensor_reduce(total[:, :], deg[:, :], AX.X, ALU.add))
            mark("totals")
            dve.wait_ge(s_tot, 1)
            step(dve.tensor_scalar(flag[:, :], ps[0:1, 0:1], float(E), None, ALU.is_equal))
            dve.sem_inc(s_flag, 1)
            fits = take_flag(dve)
            with dve.If(fits == 0):
                with dve.Fori(0, IT) as i:
                    for k in range(K):
                        onehots(slow, 0, i, k)
                dve.wait_ge(slow.mm, K + mm(1))
                dve.tensor_copy(deg[:, :], small[:, 0:NB]).then_inc(s_sv, 1)
                dve.wait_ge(s_sv, 1)
            ts(st[:, 4, :], deg[:, :], 1.0, None, ALU.add)
            mark("deg")
            ts(deg[:, :], deg[:, :], 1.0, None, ALU.max)
            step(dve.reciprocal(rdeg[:, :], deg[:, :]))
            dve.wait_ge(ready["sqrt_deg"], 1)
            step(dve.reciprocal(dinv[:, :], dinv[:, :]))
            tt(agg, cen, across(dinv[:, :]), ALU.mult)
            mark("table0")

            def sum_neighbours(n, table):
                with dve.If(fits > 0):
                    c = 0
                    for half in range(2):
                        cols = slice(half * NPAD // 2, (half + 1) * NPAD // 2)
                        for m in range(3):
                            source = table[:, cols] if m == 0 else left
                            dve.tensor_copy(parts[:, m, cols], source).then_inc(s_split[n], 1)
                            dve.wait_ge(s_split[n], c + 1)
                            c += 1
                            if m < 2:
                                dve.tensor_tensor(left, source, parts[:, m, cols], ALU.subtract).then_inc(s_split[n], 1)
                                dve.wait_ge(s_split[n], c + 1)
                                c += 1
                    dve.sem_inc(ready[f"parts{n}"], 2)
                    cast_slabs(n + 1, n + 2)
                with dve.If(fits == 0):
                    with dve.Fori(0, IT) as i:
                        for k in range(K):
                            onehots(slow, n + 1, i, k)
                    dve.wait_ge(slow.mm, K + mm(n + 2))

            sum_neighbours(0, agg.rearrange("p b d -> p (b d)"))
            tt(agg, acc[:, 0:NPAD].rearrange("p (b d) -> p b d", d=D), agg, ALU.add)
            tt(agg, agg, across(dinv[:, :]), ALU.mult)
            mark("agg0")

            def edge_term(i, s):
                for h in range(H):
                    c = 2 * h
                    dve.tensor_tensor(ea_tmp, ea_buf[:, s, :, :],
                                      U[:, h, :].unsqueeze(1).broadcast_to([P, K, ED]), ALU.mult).then_inc(s_et, 1)
                    dve.wait_ge(s_et, 8 * i + c + 1)
                    dve.tensor_reduce(EA[:, bass.ds(i, 1), h, :].rearrange("p o k -> p (o k)"), ea_tmp, AX.X, ALU.add).then_inc(s_et, 1)
                    dve.wait_ge(s_et, 8 * i + c + 2)
                dve.sem_inc(s_eau, 1)

            def take_sums(factor):
                tt(agg, acc[:, 0:NPAD].rearrange("p (b d) -> p b d", d=D), across(factor), ALU.mult)

            with dve.Fori(0, NB // 2) as i:
                for s in range(2):
                    dve.wait_ge(s_ae0, 2 * i + s + 1)
                    dve.tensor_tensor(ab[:, s, :], ps[:, s * BK:s * BK + D], gl[:, s, :], ALU.mult).then_inc(s_of, 1)
                    dve.wait_ge(s_of, OF["gcn"] + 2 * i + s + 3)
                    xb = X[:, bass.ds(2 * i + s, 1), :].rearrange("p o d -> p (o d)")
                    dve.tensor_tensor(xb, xb, ab[:, s, :], ALU.add).then_inc(s_xb, 1)
            dve.wait_ge(s_xb, NB)

            layernorm("ln1", "c1")
            ts(Hn[:, :, :], cen, 0.0, None, ALU.max)
            ts(agg, cen, 0.0, None, ALU.max)
            mark("table1")
            sum_neighbours(1, Hn[:, :, :].rearrange("p b d -> p (b d)"))
            take_sums(rdeg[:, :])
            step(dve.scalar_tensor_tensor(agg, agg, 0.5, Hn[:, :, :], ALU.mult, ALU.add))
            tt(X[:, :, :], X[:, :, :], agg, ALU.add)

            layernorm("ln2", "c2")
            ts(Hn[:, :, :], cen, 0.0, None, ALU.max)
            mark("h2")
            def take_relations(i, first=False):
                for s in range(2):
                    dve.wait_ge(s_mo, NB + 2 * i + s + 1)
                    if not first:
                        dve.wait_ge(s_t2[s], 16 * i)
                    dve.tensor_copy(cen[:, bass.ds(2 * i + s, 1), :].rearrange("p o d -> p (o d)"),
                                    ps[:, (3 * s + 2) * BK:(3 * s + 2) * BK + D]).then_inc(s_xb, 1)
                    dve.tensor_copy(t2_stage[:, s, 0:512], ps[:, 3 * s * BK:(3 * s + 1) * BK]).then_inc(s_xb, 1)
                    dve.wait_ge(s_xb, NB + 4 * i + 2 * s + 2)
                    dve.wait_ge(s_ae, 2 * i + s + 1)
                    dve.sem_inc(s_of, 1)
            take_relations(0, True)
            with dve.Fori(1, NB // 2) as i:
                take_relations(i)
            with dve.Fori(0, IT // 2) as j:
                for s in range(2):
                    for k in range(K):
                        onehots(main, 0, 2 * j + s, k)
                    dve.wait_ge(s_ea[s], 16 * j + 16)
                    edge_term(2 * j + s, s)
            for k in range(K):
                onehots(main, 0, IT - 1, k)
            dve.wait_ge(s_ea[0], 16 * (IT // 2) + 32)
            edge_term(IT - 1, 0)

            dve.wait_ge(main.mm, K + mm(1))
            take_sums(rdeg[:, :])
            tt(agg, agg, cen, ALU.add)
            ts(agg, agg, 0.0, None, ALU.max)
            tt(X[:, :, :], X[:, :, :], agg, ALU.add)

            layernorm("ln3", "c3")
            ts(Hn[:, :, :], cen, 0.0, None, ALU.max)
            mark("h3")
            with dve.Fori(0, NB // 2) as i:
                for s in range(2):
                    b = bass.ds(2 * i + s, 1)
                    dve.wait_ge(s_mo, 2 * NB + 2 * i + s + 1)
                    o = ps[:, s * BK:s * BK + D + 2 * H]
                    dve.tensor_copy(agg[:, b, :].rearrange("p o d -> p (o d)"), o[:, 0:D]).then_inc(s_xb, 1)
                    dve.tensor_copy(sdst[:, b, :].rearrange("p o d -> p (o d)"), o[:, D:D + H]).then_inc(s_xb, 1)
                    dve.tensor_copy(ssrc[:, b, :].rearrange("p o d -> p (o d)"), o[:, D + H:D + 2 * H]).then_inc(s_xb, 1)
                    dve.wait_ge(s_xb, 3 * NB + 6 * i + 3 * s + 3)
                    dve.sem_inc(s_of, 1)
            dve.wait_ge(s_of, OF["end"] + 2)
            mark("table3")
            split3(ssrc3, ssrc[:, :, :].rearrange("p b h -> p (b h)"), split_tmp[:, 0:NB * H])
            split3(sdst3, sdst[:, :, :].rearrange("p b h -> p (b h)"), split_tmp[:, :])
            mark("score_tables")

            def build(i, q, s):
                n = 4 if q < NQ - 1 else 2
                cols = slice(q * 4 * P, q * 4 * P + n * P)
                for o, w in ((ohs, 0), (ohd, 1)):
                    ins = dve.tensor_scalar(o[:, q, 0:n * P], rows[:, w, s, cols], part[:, 0:1], None, ALU.is_equal)
                ins.then_inc(s_qoh, 1)

            def pick(i, q, s):
                n = 4 if q < NQ - 1 else 2
                dve.wait_ge(s_qmm, NQ * i + q + 1)
                bank = ps[:, q * BK:(q + 1) * BK]
                pr = prod[:, q % 2, 0:n * NB * H].rearrange("p (k b h) -> p k b h", b=NB, h=H)
                dve.tensor_tensor(pr, bank[:, 0:n * NB * H].rearrange("p (k b h) -> p k b h", b=NB, h=H),
                                  hi_mask[:, s, 4 * q:4 * q + n, :].unsqueeze(3).broadcast_to([P, n, NB, H]),
                                  ALU.mult).then_inc(s_prod, 1)
                dve.tensor_copy(sd_two[:, s, 4 * q:4 * q + n, :],
                                bank[:, 4 * NB * H:4 * NB * H + n * 2 * H].rearrange("p (k w) -> p k w", w=2 * H)).then_inc(s_qd, 1)
                dve.wait_ge(s_prod, NQ * i + q + 1)
                dve.tensor_reduce(ZM[:, bass.ds(i, 1), :, 4 * q:4 * q + n].rearrange("p o h k -> p (o k) h"),
                                  pr.rearrange("p k b h -> p k h b"), AX.X, ALU.add).then_inc(s_rq, 1)

            def pass_a_step(i, s, j, more=True):
                dve.tensor_tensor(hi_mask[:, s, :, :],
                                  hi[:, bass.ds(i * K, K)].unsqueeze(2).broadcast_to([P, K, NB]),
                                  wide[:, 0:NB].unsqueeze(1).broadcast_to([P, K, NB]), ALU.is_equal).then_inc(s_hm, 1)
                dve.tensor_scalar(in_block[:, s, 0, :], rel[:, bass.ds(i * K, K)], float(P), None, ALU.is_lt).then_inc(s_hm, 1)
                dve.tensor_scalar(in_block[:, s, 1, :], rel[:, bass.ds(i * K, K)], float(P), None, ALU.is_ge).then_inc(s_hm, 1)
                if more:
                    dve.wait_ge(s_row[1 - s], 32 * (j + s) + 32)
                dve.wait_ge(s_hm, 3 * i + 3)
                for q in range(NQ):
                    pick(i, q, s)
                    if more:
                        build(i + 1, q, 1 - s)
                dve.wait_ge(s_qd, NQ * (i + 2))
                two = sd_two[:, s, :, :].rearrange("p k (w h) -> p w h k", w=2)
                for w in range(2):
                    dve.tensor_tensor(two[:, w], two[:, w],
                                      in_block[:, s, w, :].unsqueeze(1).broadcast_to([P, H, K]), ALU.mult).then_inc(s_pr, 1)
                if more:
                    dve.wait_ge(s_qoh, NQ * (i + 2))
                    dve.sem_inc(s_rowu, 1)
                dve.wait_ge(s_pr, 3 * i + 2)
                dve.tensor_tensor(SD[:, bass.ds(i, 1), :, :].rearrange("p o h k -> p (o h) k"),
                                  two[:, 0], two[:, 1], ALU.add).then_inc(s_pr, 1)

            dve.wait_ge(s_row[0], 32)
            for q in range(NQ):
                build(0, q, 0)
            dve.wait_ge(s_qoh, NQ)
            dve.sem_inc(s_rowu, 1)
            with dve.Fori(0, IT // 2) as j:
                for s in range(2):
                    pass_a_step(2 * j + s, s, j)
            pass_a_step(IT - 1, 0, IT // 2, more=False)
            dve.wait_ge(s_pr, 3 * IT)
            dve.wait_ge(s_rq, 7 * IT)
            dve.wait_ge(s_tabr, 16)
            tt(EA[:, :, :, :], EA[:, :, :, :], ZM[:, :, :, :], ALU.add)
            step(dve.memset(dt_.bitcast(I32)[0:RG, (IT - 1) * P:IT * P], PAD_NODE))
            mark("dst_pads")

            def from_scores(i, s):
                return dve.tensor_copy(stage[:, s, 0:RG], EA[:, bass.ds(i, 1), :, :].rearrange("p o h k -> p (o h k)"))

            def from_maxima(i, s):
                return dve.tensor_copy(stage[0:RG, s, :], bw[0:RG, bass.ds(i * P, P)])

            def stage_all(copy, base):
                for s in range(2):
                    copy(s, s).then_inc(s_zs, 1)
                with dve.Fori(1, IT // 2) as j:
                    for s in range(2):
                        dve.wait_ge(s_zt, base + 2 * j + s - 1)
                        copy(2 * j + s, s).then_inc(s_zs, 1)
                dve.wait_ge(s_zt, base + IT - 2)
                copy(IT - 1, 0).then_inc(s_zs, 1)

            stage_all(from_scores, 0)
            dve.wait_ge(s_ztc, 2 + IT)
            dve.wait_ge(s_dt, 16 * 3 * H)
            d3 = dt_[0:RG, :].rearrange("r (i e) -> r i e", e=P)
            b3 = brk[0:RG, :].rearrange("r (i e) -> r i e", e=P)
            f3 = fw[0:RG, :].rearrange("r (i e) -> r i e", e=P)
            w3 = bw[0:RG, :].rearrange("r (i e) -> r i e", e=P)
            step(dve.tensor_copy(fw[0:RG, :], dt_[0:RG, :].bitcast(I32)))
            step(dve.tensor_copy(dt_[0:RG, :], fw[0:RG, :]))
            step(dve.memset(b3[:, :, 0:1], -BIG))
            tt(b3[:, :, 1:P], d3[:, :, 1:P], d3[:, :, 0:P - 1], ALU.not_equal)
            ts(b3[:, :, 1:P], b3[:, :, 1:P], -BIG, None, ALU.mult)
            step(dve.tensor_tensor_scan(fw[0:RG, :], brk[0:RG, :], zt[0:RG, :], -BIG, ALU.add, ALU.max))
            step(dve.memset(b3[:, :, P - 1:P], -BIG))
            tt(b3[:, :, 0:P - 1], d3[:, :, 1:P], d3[:, :, 0:P - 1], ALU.not_equal)
            ts(b3[:, :, 0:P - 1], b3[:, :, 0:P - 1], -BIG, None, ALU.mult)
            step(dve.tensor_tensor_scan(bw[0:RG, ::-1], brk[0:RG, ::-1], zt[0:RG, ::-1], -BIG, ALU.add, ALU.max))
            step(dve.tensor_copy(ends_sb[:, 0, :].unsqueeze(2), f3[:, :, P - 1:P]))
            step(dve.tensor_copy(ends_sb[:, 1, :].unsqueeze(2), w3[:, :, 0:1]))
            tt(ends_sb[:, 2, :].unsqueeze(2), d3[:, :, 0:1], d3[:, :, P - 1:P], ALU.is_equal)
            step(dve.tensor_copy(ends_sb[:, 3, :].unsqueeze(2), d3[:, :, 0:1]))
            step(dve.tensor_copy(ends_sb[:, 4, :].unsqueeze(2), d3[:, :, P - 1:P]))
            mark("ends_cols")
            dve.wait_ge(s_ect, 1)
            for q in range(5):
                step(dve.tensor_copy(ends_t[:, q, :], ps[0:IT, q * BK:q * BK + RG]))
            mark("ends")
            dve.wait_ge(s_ends, 16 * 6)
            step(dve.memset(ch[:, 5, 0:1], 0.0))
            tt(ch[:, 5, 1:T], ch[:, 3, 1:T], ch[:, 4, 0:T - 1], ALU.is_equal)
            tt(ch[:, 6, :], ch[:, 5, :], ch[:, 2, :], ALU.mult)
            ts(ch[:, 6, :], ch[:, 6, :], 1.0, BIG, ALU.subtract, ALU.mult)
            step(dve.tensor_tensor_scan(ch[:, 0, :], ch[:, 6, :], ch[:, 0, :], -BIG, ALU.add, ALU.max))
            step(dve.memset(ch[:, 6, T - 1:T], -BIG))
            tt(ch[:, 6, 0:T - 1], ch[:, 5, 1:T], ch[:, 2, 0:T - 1], ALU.mult)
            ts(ch[:, 6, 0:T - 1], ch[:, 6, 0:T - 1], 1.0, BIG, ALU.subtract, ALU.mult)
            step(dve.tensor_tensor_scan(ch[:, 1, ::-1], ch[:, 6, ::-1], ch[:, 1, ::-1], -BIG, ALU.add, ALU.max))
            ts(ch[:, 5, :], ch[:, 5, :], 1.0, BIG, ALU.subtract, ALU.mult)
            step(dve.memset(ch[:, 7, 0:1], -BIG))
            tt(ch[:, 7, 1:T], ch[:, 0, 0:T - 1], ch[:, 5, 1:T], ALU.add)
            step(dve.memset(ch[:, 8, T - 1:T], -BIG))
            tt(ch[:, 8, 0:T - 1], ch[:, 1, 1:T], ch[:, 5, 1:T], ALU.add)
            mark("carries")
            dve.wait_ge(s_ends, 16 * 9)
            mark("carries_read")
            dve.wait_ge(s_ect, 2)
            for q in range(2):
                step(dve.tensor_copy(car_in[:, q, :], ps[0:RG, q * BK:q * BK + IT]))
            for q, o, c in ((0, f3, 3), (1, w3, 4)):
                tt(b3, d3, across(ends_sb[:, c, :], P), ALU.not_equal)
                ts(b3, b3, -BIG, None, ALU.mult)
                tt(b3, b3, across(car_in[:, q, :], P), ALU.add)
                tt(o, o, b3, ALU.max)
            tt(w3, w3, f3, ALU.max)
            stage_all(from_maxima, IT)
            dve.wait_ge(s_ztc, 2 + 2 * IT)

            tt(ZM[:, :, :, :], ZM[:, :, :, :], SD[:, :, :, :], ALU.add)
            step(dve.scalar_tensor_tensor(zmf, zmf, 0.2, zmf, ALU.mult, ALU.max))
            tt(EA[:, :, :, :], EA[:, :, :, :], SD[:, :, :, :], ALU.add)
            step(dve.scalar_tensor_tensor(eaf, eaf, 0.2, eaf, ALU.mult, ALU.max))
            tt(EA[:, :, :, :], EA[:, :, :, :], ZM[:, :, :, :], ALU.subtract)
            mark("alpha")
            dve.wait_ge(ready["exp"], 1)
            split3(E3, eaf, zt[:, 0:T * H])
            mark("weights3")

            with dve.Fori(0, IT) as i:
                for k in range(K):
                    onehots(main, 1, i, k)
                    dve.tensor_scalar(oh_b[:, k, :], wide_b[:, :], rel[:, bass.ds(i * K + k, 1)], None, ALU.is_equal)
                    if k % HK == 0:
                        dve.wait_ge(s_eb, 2 * i + k // HK + 1)
                    main.wait_gathered(dve, k, 1, i)
                    dve.tensor_tensor(xw[:, k, :].rearrange("p (h c) -> p h c", c=C),
                                      xg[:, k, :].rearrange("p (h c) -> p h c", c=C),
                                      e_buf[:, k // HK, k % HK, :].unsqueeze(2).broadcast_to([P, H, C]),
                                      ALU.mult).then_inc(s_xw, 1)
            dve.wait_ge(main.mm, K + mm(2))
            den3 = small[:, 0:NB * 3 * H].rearrange("p (b n h) -> p b h n", n=3, h=H)
            step(dve.tensor_reduce(den[:, :, :], den3, AX.X, ALU.add))
            ts(den[:, :, :], den[:, :, :], 1e-16, None, ALU.add)
            step(dve.reciprocal(rden[:, :, :], den[:, :, :]))
            tt(agg.rearrange("p b (h c) -> p (b h) c", c=C), acc[:, 0:NPAD].rearrange("p (n c) -> p n c", c=C),
               rden[:, :, :].rearrange("p b h -> p (b h)").unsqueeze(2).broadcast_to([P, NB * H, C]), ALU.mult)

            def over_blocks(n):
                return vecs[:, n, :].unsqueeze(1).broadcast_to([P, NB, D])
            tt(agg, agg, over_blocks(0), ALU.add)
            tt(agg, agg, Hn[:, :, :], ALU.add)
            layernorm("ln4", "c4")
            tt(cen, cen, over_blocks(1), ALU.mult)
            tt(cen, cen, over_blocks(2), ALU.add)
            ts(agg, cen, 0.0, None, ALU.min)
            mark("elu_min")
            dve.wait_ge(ready["elu_exp"], 1)
            ts(cen, cen, 0.0, None, ALU.max)
            step(dve.scalar_tensor_tensor(cen, sq, -1.0, cen, ALU.add, ALU.add))
            tt(X[:, :, :], X[:, :, :], cen, ALU.add)
            mark("final")

        @block.tensor
        def _(pe):
            for r in (slow, main):
                pe.sem_inc(r.mm, K)
            pe.sem_inc(s_pm, NP)
            for n in range(2):
                pe.sem_inc(s_su[n], 1)

            pe.wait_ge(ready["index_rows"], 1)
            for n, r in enumerate(rows_f):
                for g in range(G):
                    m = RG if g < G - 1 else GL
                    c = n * G + g
                    if c >= 8:
                        pe.wait_ge(s_tc, c - 7)
                    pe.transpose(ps[:, (c % 8) * BK:(c % 8) * BK + m], r[0:m, g, :], ident[0:m, 0:m]).then_inc(s_t, 1)

            pe.wait_ge(ready["bases"], 1)
            pe.matmul(ps[:, 0:T // 2], ones[0:1, :], base_f[:, :], start=True, stop=True).then_inc(s_bc, 1)

            pe.wait_ge(ready["att"], 1)
            pe.transpose(ps[:, 0:D], WSn[:, :], ident[:, :])
            pe.transpose(ps[:, BK:BK + D], WLn[:, :], ident[:, :])
            pe.matmul(ps[:, 2 * BK:2 * BK + 2 * H], WLn[:, :], att3[:, 0:2, :].rearrange("p n h -> p (n h)"), start=True, stop=True)
            for h in range(H):
                last = pe.matmul(ps[:, 3 * BK + h * ED:3 * BK + (h + 1) * ED], att_wide[:, h, :], WE[:, :], start=True, stop=True)
            last.then_inc(s_pe0, 1)
            pe.wait_ge(ready["weights"], 1)
            pe.wait_ge(s_b0, 16)

            def load_blocks(i, k):
                return nc.values_load_multi_w_load_instructions(
                    b0_row[0:1, bass.ds(i, 1), k:k + 4].rearrange("p o k -> p (o k)"),
                    engines=(PE,), min_val=0, max_val=NB - 2,
                    skip_runtime_bounds_check_because="blocks are below NB - 1")[1]

            def zero_psum():
                for b in range(8):
                    last = pe.matmul(ps[:, b * BK:(b + 1) * BK], zero_w[:, :], zeros[:, :], start=True, stop=True)

            def add_tiles(r, n, m, kind):
                zero_psum()
                with pe.Fori(0, IT) as i:
                    for k in range(K):
                        if k % 4 == 0:
                            regs = load_blocks(i, k)
                        b = regs[k % 4]
                        if kind == "weighted":
                            pe.wait_ge(s_xw, i * K + k + 1)
                        else:
                            pe.wait_ge(r.oh, mm(n) + i * K + k + 1)
                            if kind == "rows":
                                r.wait_gathered(pe, k, m, i)
                        for w in range(2):
                            one = oh[:, k, w * P:(w + 1) * P]
                            if kind == "count":
                                last = pe.matmul(small[:, bass.ds(b + w, 1)], one, ones[:, 0:1],
                                                 start=False, stop=False, skip_group_check=True)
                                continue
                            last = pe.matmul(acc[:, bass.ds(b * P + w * P, P)], one,
                                             (xw if kind == "weighted" else xg)[:, k, :],
                                             start=False, stop=False, skip_group_check=True)
                            if kind == "weighted":
                                last = pe.matmul(small[:, bass.ds(b * (3 * H) + w * (3 * H), 3 * H)],
                                                 oh_b[:, k, w * P:(w + 1) * P], e3_buf[:, k // HK, k % HK, :],
                                                 start=False, stop=False, skip_group_check=True)
                        last.then_inc(r.mm, 1)

            def with_counts(n, product):
                zero_psum()
                with pe.Fori(0, HI) as b:
                    row = nc.tensor.snap(b * P)
                    for h in range(2):
                        pe.wait_ge(s_sl[h], n * HI + b + 1)
                        for c in range(SLAB[h] // P):
                            last = product(slabs[h][:, c * P:(c + 1) * P], c + h * (SLAB[0] // P), row)
                        last.then_inc(s_su[h], 1)

            def degrees(block_counts, c, row):
                return pe.matmul(small[:, c:c + 1], block_counts, ones_b[:, :], start=False, stop=False, skip_group_check=True)

            def sums(block_counts, c, row):
                for m in range(3):
                    last = pe.matmul(acc[:, c * P:(c + 1) * P], block_counts, parts[:, m, bass.ds(row, P)],
                                     start=False, stop=False, skip_group_check=True)
                return last

            def sum_neighbours(n):
                with pe.If(fits > 0):
                    pe.wait_ge(ready[f"parts{n}"], 1)
                    with_counts(n + 1, sums)
                    pe.drain().then_inc(s_dense, 1)
                with pe.If(fits == 0):
                    add_tiles(slow, n + 1, n, "rows")

            def multiply_blocks(n, bank_of, product):
                with pe.Fori(0, NB // 2) as i:
                    for s in range(2):
                        pe.wait_ge(s_st, NB * n + 2 * i + s + 1)
                        pe.transpose(turned[s], stage[:, s, :], ident[:, :]).then_inc(s_tp, 1)
                    for s in range(2):
                        pe.wait_ge(s_lt, NB * n + 2 * i + s + 1)
                        pe.wait_ge(s_of, NB * n + 2 * i + s + 1)
                        product(s, bank_of * s * BK).then_inc(s_mo, 1)

            def gcn(s, o):
                pe.matmul(ps[:, o:o + 2 * D], ones[0:1, :], B0[:, :], start=True, stop=False)
                return pe.matmul(ps[:, o:o + 2 * D], lt[:, s, :], W0[:, :], start=False, stop=True)

            def relations(s, o):
                for c in range(2):
                    pe.matmul(ps[:, o + c * BK:o + (c + 1) * BK], lt[:, s, :],
                              WR[:, 4 * c:4 * c + 4, :].rearrange("p r d -> p (r d)"), start=True, stop=True)
                pe.matmul(ps[:, o + 2 * BK:o + 2 * BK + D], ones[0:1, :], BS[:, :], start=True, stop=False)
                return pe.matmul(ps[:, o + 2 * BK:o + 2 * BK + D], lt[:, s, :], WS[:, :], start=False, stop=True)

            def attention(s, o):
                return pe.matmul(ps[:, o:o + D + 2 * H], lt[:, s, :], WL[:, :], start=True, stop=True)

            with pe.Fori(0, IT) as i:
                for p in range(NP):
                    pe.wait_ge(s_po, NP * i + p + 1)
                    free = NP * i + p + 1 + (8 if p < NP - 8 else 0 if p < 8 else NP - 8)
                    pe.wait_ge(s_pa, free)
                    for k in range(2):
                        last = pe.matmul(ps[:, (p % 8) * BK:(p % 8) * BK + HI * W], src_oh[:, 2 * p + k, :],
                                         pair_oh[k][:, p, :], start=(k == 0), stop=(k == 1))
                    last.then_inc(s_pm, 1)
            pe.wait_ge(ready["counted"], 1)
            with_counts(0, degrees)
            pe.drain().then_inc(s_dense, 1)
            pe.wait_ge(ready["totals"], 1)
            pe.matmul(ps[0:1, 0:1], total[:, :], ones[:, 0:1], start=True, stop=True).then_inc(s_tot, 1)
            fits = take_flag(pe)
            with pe.If(fits == 0):
                add_tiles(slow, 0, 0, "count")
            pe.wait_ge(ready["table0"], 1)
            sum_neighbours(0)
            multiply_blocks(0, 1, gcn)
            pe.wait_ge(ready["table1"], 1)
            sum_neighbours(1)
            pe.wait_ge(ready["h2"], 1)
            multiply_blocks(1, 3, relations)
            pe.wait_ge(s_of, OF["att"] + 2)
            add_tiles(main, 0, 0, "rows")
            pe.wait_ge(ready["h3"], 1)
            multiply_blocks(2, 1, attention)

            pe.wait_ge(ready["score_tables"], 1)
            pe.wait_ge(s_of, OF["end"] + 2)

            with pe.Fori(0, IT) as i:
                for q in range(NQ):
                    n = 4 if q < NQ - 1 else 2
                    regs = load_blocks(i, 4 * q)
                    pe.wait_ge(s_qoh, NQ * i + q + 1)
                    pe.wait_ge(s_qd, NQ * i + q + 1)
                    for kk in range(n):
                        o = q * BK + kk * NB * H
                        for part3 in range(3):
                            pe.matmul(ps[:, o:o + NB * H], ohs[:, q, kk * P:(kk + 1) * P], ssrc3[:, part3, :],
                                      start=(part3 == 0), stop=(part3 == 2))
                        o = q * BK + 4 * NB * H + kk * 2 * H
                        b = nc.tensor.snap(regs[kk] * H)
                        for part3 in range(3):
                            last = pe.matmul(ps[:, o:o + 2 * H], ohd[:, q, kk * P:(kk + 1) * P],
                                             sdst3[:, part3, bass.ds(b, 2 * H)], start=(part3 == 0), stop=(part3 == 2))
                    last.then_inc(s_qmm, 1)

            def turn(base, cols):
                def one(i, s):
                    pe.wait_ge(s_zs, base + i + 1)
                    pe.wait_ge(s_ztc, base + i + 1)
                    if cols:
                        pe.transpose(ps[0:RG, s * BK:s * BK + P], stage[:, s, 0:RG], ident[:, :]).then_inc(s_zt, 1)
                    else:
                        pe.transpose(ps[:, s * BK:s * BK + RG], stage[0:RG, s, :], ident[0:RG, 0:RG]).then_inc(s_zt, 1)
                with pe.Fori(0, IT // 2) as j:
                    for s in range(2):
                        one(2 * j + s, s)
                one(IT - 1, 0)

            pe.wait_ge(s_qd, NQ + NQ * IT)
            turn(0, True)
            pe.wait_ge(ready["ends_cols"], 1)
            for q in range(5):
                last = pe.transpose(ps[0:IT, q * BK:q * BK + RG], ends_sb[:, q, :], ident[0:RG, 0:RG])
            last.then_inc(s_ect, 1)
            pe.wait_ge(ready["carries_read"], 1)
            for q in range(2):
                last = pe.transpose(ps[0:RG, q * BK:q * BK + IT], car_t[:, q, :], ident[0:IT, 0:IT])
            last.then_inc(s_ect, 1)
            turn(IT, False)
            pe.wait_ge(ready["exp"], 1)
            add_tiles(main, 1, 1, "weighted")


_INS = ['x', 'src', 'dst', 'edge_attr_16', 'edge_type_8', 'L0_gnn_W', 'L0_gnn_b', 'L2_gnn_W_rel', 'L2_gnn_W_self_w',
        'L2_gnn_W_self_b', 'L3_gnn_W_lin', 'L3_gnn_W_edge', 'L3_gnn_att_src', 'L3_gnn_att_dst', 'L3_gnn_att_edge',
        'L3_gnn_bias', 'L3_gnn_ln_gamma', 'L3_gnn_ln_beta']
_OUTS = [((3125, 128), 'float32')]


def kernel(**inputs):
    import numpy as _np
    import concourse.bacc as _bacc
    from concourse import mybir as _mybir
    from concourse.bass_utils import run_bass_kernel_spmd as _run

    nc = _bacc.Bacc("TRN2", target_bir_lowering=False, num_devices=1)
    arrays, args = {}, []
    for name in _INS:
        a = _np.ascontiguousarray(inputs[name])
        arrays[f"in_{name}_dram"] = a
        args.append(nc.dram_tensor(f"in_{name}_dram", a.shape, _mybir.dt.from_np(a.dtype), kind="ExternalInput").ap())
    for i, (shape, dtype) in enumerate(_OUTS):
        dt = _mybir.dt.from_np(_np.dtype(dtype))
        args.append(nc.dram_tensor(f"out_{i}_dram", shape, dt, kind="ExternalOutput").ap())
    build(nc, *args)
    r = _run(nc, [arrays], core_ids=[0])
    got = tuple(r.results[0][f"out_{i}_dram"] for i in range(len(_OUTS)))
    return got[0]
```

```python
import concourse.bass as bass
from concourse import mybir
from contextlib import ExitStack

FP = mybir.dt.float32
BF = mybir.dt.bfloat16
F16 = mybir.dt.float16
U8 = mybir.dt.uint8
I32 = mybir.dt.int32
ALU = mybir.AluOpType
ACT = mybir.ActivationFunctionType
AX = mybir.AxisListType
PE = mybir.EngineType.PE
DVE = mybir.EngineType.DVE

P = 128
N = 3125
D = 128
E = 103125
H, C = 4, 32
ED = 16
R = 8
NB = 26
NPAD = NB * P
K = 26
IT = 31
T = K * IT
HK = K // 2
NQ = 7
NM = 4
RG = 4 * K
G = 8
GL = T - (G - 1) * RG
TAIL = E - (T - 1) * P
PAD_NODE = 25 * P - 1
ARENA = 6 * NPAD + 3 * K * ED + 3 * T * H
BIG = 1.0e37
APART = 1.0e34
EPS = 1e-5
W_ALL = 16 * 13
OF = {"gcn": 0, "rel": NB, "att": 2 * NB, "end": 3 * NB}
PARTS = (slice(0, 14), slice(14, NB))
FIRST = 2
WEIGHTS = (slice(0, FIRST * H * K), slice(FIRST * H * K, T * H))
FULL = N // P
REST = N - FULL * P


NP = K // 2
W = 14
HI = 25
BW = HI * P
BY_ACT = [1, 4, 6, 9, 11]
BY_POOL = [p for p in range(NP) if p not in BY_ACT]
SLAB = (12 * P, 13 * P)


def mm(n):
    return n * T


class Ring:

    def __init__(self, name, sem, share):
        self.oh = sem(name + "_onehot_ready")
        self.mm = sem(name + "_tile_added")
        self.ix = sem(name + "_index_chunk_copied")
        self.share = share
        self.g = [sem(f"{name}_gathered{k}") for k in range(K // share)]

    def wait_gathered(self, eng, k, m, i):
        if k % self.share == 0:
            eng.wait_ge(self.g[k // self.share], 16 * self.share * (m * IT + i + 1))


def build(nc, x, src, dst, ea, et, w0, b0, wrel, wself, bself, wlin, wedge, attsrc, attdst, attedge,
          bias, gamma, beta, out):
    ctx = ExitStack()
    with ctx:
        def sb(name, shape, dt=FP):
            return ctx.enter_context(nc.sbuf_tensor(name, shape, dt))

        def sem(name):
            return ctx.enter_context(nc.semaphore(name))

        def dram(name, shape, dt=FP):
            return nc.dram_tensor(name, shape, dt, kind="Internal").ap()

        tab = [dram(f"tab{n}", (NPAD, D)) for n in (0, 1)]
        tab2 = dram("tab2", (NPAD * R, D))
        tab3 = dram("tab3", (NPAD, D))
        score_tab = dram("score_tab", (NPAD, H))
        tabs = [tab[0], tab[1], tab2, tab3]
        block_lin = dram("block_lin", (T, 2), I32)
        src_lo_row = dram("src_lo_row", (T * P,), BF)
        dst_lo_row = dram("dst_lo_row", (T * P,), BF)
        ends = dram("ends", (5, H, T))
        carries = dram("carries", (2, H, T))

        X = sb("X", [P, NB, D])
        Hn = sb("Hn", [P, NB, D])
        arena = sb("arena", [P, ARENA])
        at = 0

        def carve(n):
            nonlocal at
            at += n
            assert at <= ARENA
            return arena[:, at - n:at]
        agg = carve(NPAD).rearrange("p (b d) -> p b d", d=D)
        cen = carve(NPAD).rearrange("p (b d) -> p b d", d=D)
        oh = carve(K * 256).rearrange("p (k w) -> p k w", w=256)
        xg = carve(K * D).rearrange("p (k d) -> p k d", d=D)
        xw = carve(K * D).rearrange("p (k d) -> p k d", d=D)
        ea_buf = carve(2 * K * ED).rearrange("p (s k f) -> p s k f", s=2, f=ED)
        ea_tmp = carve(K * ED).rearrange("p (k f) -> p k f", f=ED)
        EA = carve(T * H).rearrange("p (i h k) -> p i h k", h=H, k=K)
        SDZM = carve(2 * T * H)
        count = arena[:, ARENA - HI * BW // 4:ARENA].bitcast(U8).rearrange("p (b d) -> p b d", d=BW)
        parts = arena[:, NPAD:NPAD + 3 * NPAD // 2].bitcast(BF).rearrange("p (n d) -> p n d", n=3)
        left = arena[:, NPAD + 3 * NPAD // 2:3 * NPAD]
        slab_at = (0, SLAB[0] // 2)
        slabs = [left[:, slab_at[n]:slab_at[n] + SLAB[n] // 2].bitcast(BF) for n in range(2)]
        deg_row = arena[0:1, 0:BW]
        src_oh = arena[:, 2 * NPAD:2 * NPAD + K * P // 2].bitcast(BF).rearrange("p (k n) -> p k n", k=K)
        pair_at = (0, 2 * NPAD + K * P // 2)
        at = pair_at[1] + NP * HI * W // 2
        slo_buf = carve(K)
        slo_act = carve(K)
        away = carve(P).bitcast(BF).rearrange("p (k n) -> p k n", k=2)
        assert at <= ARENA - HI * BW // 4
        pair_oh = [arena[:, a:a + NP * HI * W // 2].bitcast(BF).rearrange("p (s n) -> p s n", s=NP) for a in pair_at]
        sq = oh.rearrange("p k w -> p (k w)")[:, 0:NPAD].rearrange("p (b d) -> p b d", d=D)
        t2_stage = xg.rearrange("p k d -> p (k d)")[:, 0:2 * R * D].rearrange("p (s n) -> p s n", s=2)
        at = 0
        SROW = IT * P
        fw = carve(SROW)
        bw = carve(SROW)
        dt_ = carve(SROW)
        chains_at = at
        zt = carve(SROW)
        brk = carve(SROW)
        ch = arena[0:H, chains_at:chains_at + 9 * T].rearrange("h (q t) -> h q t", t=T)
        at = NPAD
        rows = carve(4 * K * P // 2).bitcast(BF).rearrange("p (w s n) -> p w s n", w=2, s=2)
        ohs = carve(NQ * 2 * P).bitcast(BF).rearrange("p (s n) -> p s n", s=NQ)
        ohd = carve(NQ * 2 * P).bitcast(BF).rearrange("p (s n) -> p s n", s=NQ)
        hi_mask = carve(2 * 4 * NM * NB).rearrange("p (s k b) -> p s k b", s=2, b=NB)
        prod = carve(2 * 4 * NB * H).rearrange("p (s n) -> p s n", s=2)
        sd_two = carve(2 * K * 2 * H).rearrange("p (s k w) -> p s k w", s=2, w=2 * H)
        sg = carve(2 * (NQ - NM) * 4 * H).rearrange("p (s q k h) -> p s q k h", s=2, k=4, h=H)
        sg_idx = carve(2 * (K - 4 * NM)).bitcast(I32).rearrange("p (s k) -> p s k", s=2)
        bh_row = carve(IT * 28)[0:1].bitcast(I32).rearrange("p (i k) -> p i k", i=IT)
        at = NPAD * 2
        rows_i = [carve(G * P).bitcast(I32).rearrange("p (g e) -> p g e", e=P) for _ in range(3)]
        rows_f = [carve(G * P).rearrange("p (g e) -> p g e", e=P) for _ in range(5)]
        lo_i = carve(G * P).bitcast(I32).rearrange("p (g e) -> p g e", e=P)
        lo_b = [carve(G * P // 2).bitcast(BF).rearrange("p (g e) -> p g e", e=P) for _ in range(2)]

        rel = sb("rel", [P, T])
        hi = sb("hi", [P, T])
        idx = sb("idx", [P, T], I32)
        hidx = sb("hidx", [P, T], I32)
        idx_buf = sb("idx_buf", [P, K], I32)
        SD, ZM = (SDZM[:, n * T * H:(n + 1) * T * H].rearrange("p (i h k) -> p i h k", h=H, k=K) for n in range(2))
        code = sb("code", [P, T])
        slo = sb("slo", [P, T])
        base_row = sb("base_row", [1, T // 2], I32)
        base_f = arena[0:1, 2 * T:2 * T + T // 2]
        io_c = sb("io_c", [P, HI * W], I32)
        wide_c = sb("wide_c", [P, HI * W], F16)
        total = sb("total", [1, 1])
        flag = sb("flag", [1, 1], I32)
        ones_b = sb("ones_b", [P, 1], BF)
        inside = agg.rearrange("p b d -> p (b d)")[:, 0:T]
        in_tmp = agg.rearrange("p b d -> p (b d)")[:, T:2 * T]
        b0_lin = sb("b0_lin", [RG, G, 2], I32)
        b0_f = sb("b0_f", [RG, G])
        b0_row = sb("b0_row", [1, IT, 28, 2], I32)

        io_p = sb("io_p", [P, 1], I32)
        io_w = sb("io_w", [P, 256], I32)
        part = sb("part", [P, 1])
        wide = sb("wide", [P, 256])
        wide_b = sb("wide_b", [P, 256], BF)
        ident = sb("ident", [P, P])
        ones = sb("ones", [P, P])
        zeros = sb("zeros", [P, 512], BF)
        zero_w = sb("zero_w", [P, P], BF)
        deg = sb("deg", [P, NB])
        dinv = sb("dinv", [P, NB])
        rdeg = sb("rdeg", [P, NB])
        st = sb("st", [P, 6, NB])
        stage = sb("stage", [P, 2, P])
        lt = sb("lt", [P, 2, P])
        ab = sb("ab", [P, 2, P])
        gl = sb("gl", [P, 2, P])
        W0 = sb("W0", [P, 2 * D])
        B0 = sb("B0", [1, 2 * D])
        WR = sb("WR", [P, R, D])
        WSn = sb("WSn", [P, D])
        WS = sb("WS", [P, D])
        BS = sb("BS", [1, D])
        WLn = sb("WLn", [P, D])
        WL = sb("WL", [P, D + 2 * H])
        WE = sb("WE", [P, ED])
        att = sb("att", [P, 3])
        head = sb("head", [P, H])
        att3 = sb("att3", [P, 3, H])
        att_wide = sb("att_wide", [P, H, P])
        U = sb("U", [P, H, ED])
        vecs = sb("vecs", [P, 3, D])
        ssrc = sb("ssrc", [P, NB, H])
        sdst = sb("sdst", [P, NB + 1, H])
        den = sb("den", [P, NB, H])
        ssrc3 = sb("ssrc3", [P, 3, NB * H], BF)
        sdst3 = sb("sdst3", [P, NB + 1, 3, H], BF)
        split_tmp = sb("split_tmp", [P, (NB + 1) * H])
        ends_sb = sb("ends_sb", [RG, 5, IT])
        ends_t = sb("ends_t", [IT, 5, RG])
        car_t = sb("car_t", [IT, 2, RG])
        car_in = sb("car_in", [RG, 2, IT])
        rden = sb("rden", [P, NB, H])
        in_block = sb("in_block", [P, 2, 2, K])
        e_buf = sb("e_buf", [P, 2, HK, H])
        e3_buf = sb("e3_buf", [P, 2, HK, 3 * H], BF)
        E3 = SDZM[:, 0:3 * T * H // 2].bitcast(BF).rearrange("p (n t) -> p n t", n=3)
        oh_b = agg.rearrange("p b d -> p (b d)").bitcast(BF).rearrange("p (k w) -> p k w", w=2 * P)

        ps = ctx.enter_context(nc.psum_tensor("ps", [P, 4096], FP))
        BK = 512
        acc = ps[:, 0:7 * BK]
        small = ps[:, 7 * BK:8 * BK]
        turned = [ps[:, (6 + s) * BK:(6 + s) * BK + P] for s in range(2)]

        s_rows = sem("index_rows_loaded")
        s_x = sem("x_loaded")
        s_w = sem("weights_loaded")
        s_io = sem("iotas_written")
        s_v = sem("vector_steps")
        s_a = sem("scalar_steps")
        s_t = sem("index_turned")
        s_tc = sem("index_copied")
        s_scr = sem("index_scratch_written")
        s_b0 = sem("block_row_loaded")
        s_pe0 = sem("weights_turned")
        slow, main = Ring("slow", sem, HK), Ring("main", sem, 2)
        s_tabr = sem("table_ready")
        s_ea = [sem(f"edge_attr_loaded{k}") for k in range(2)]
        s_eau = sem("edge_attr_used")
        s_xw = sem("rows_weighted")
        s_st = sem("block_staged")
        s_tp = sem("block_turned")
        s_lt = sem("turned_copied")
        s_mo = sem("block_multiplied")
        s_of = sem("block_taken")
        s_ae = sem("act_block_out")
        s_t2 = [sem(f"tab2_block_written{k}") for k in range(2)]
        s_row = [sem(f"lo_rows_loaded{k}") for k in range(2)]
        s_rowu = sem("lo_rows_used")
        s_qoh = sem("quad_onehots")
        s_qmm = sem("quad_picked")
        s_zs = sem("scores_staged")
        s_zt = sem("scores_turned")
        s_ztc = sem("scores_turned_copied")
        s_dt = sem("dst_rows_loaded")
        s_ends = sem("ends_moved")
        s_out = sem("out_written")
        s_et = sem("edge_term_steps")
        s_ae0 = sem("gelu_block")
        s_xb = sem("block_added")
        s_hm = sem("hi_mask_written")
        s_pr = sem("quad_steps")
        s_qd = sem("quad_psum_read")
        s_eb = sem("weights_staged")
        s_base = sem("pair_bases_loaded")
        s_bc = sem("pair_bases_spread")
        s_cnt0 = sem("counts_zeroed")
        s_po = sem("pair_onehots")
        s_so = sem("source_onehots")
        s_ao = sem("source_onehots_by_act")
        s_away = sem("distances_written")
        s_sla = sem("source_columns_copied_by_act")
        s_slo = sem("source_columns_copied")
        s_pm = sem("pair_multiplied")
        s_pa = sem("pair_added")
        s_sl = [sem(f"slab_ready{n}") for n in range(2)]
        s_su = [sem(f"slab_used{n}") for n in range(2)]
        s_tot = sem("degrees_turned")
        s_flag = sem("flag_written")
        s_sv = sem("vector_steps_slow")
        s_dense = sem("dense_sums_done")
        s_split = [sem(f"table_split{n}") for n in range(2)]
        s_tabs = sem("slow_table_ready")
        s_stab = sem("score_table_ready")
        s_sgi = sem("score_indices_copied")
        s_sg = [[sem(f"scores_gathered{s}{q}") for q in range(NQ - NM)] for s in range(2)]
        s_prod = sem("quad_masked")
        s_rq = sem("reduced")
        s_ect = sem("ends_turned")
        s_held = sem("pool_waits_over")
        zmf = ZM[:, :, :, :].rearrange("p i h k -> p (i h k)")
        eaf = EA[:, :, :, :].rearrange("p i h k -> p (i h k)")
        ready = {m: sem("ready_" + m) for m in (
            "pads_set index_rows index_cols att weights c0 c0_var h0 ln0_sq ln0_std deg sqrt_deg table0 agg0 "
            "c1 c1_var ln1_sq ln1_std table1 c2 c2_var ln2_sq ln2_std h2 c3 c3_var ln3_sq ln3_std h3 table3 "
            "dst_pads ends_cols ends carries carries_read ring_free alpha exp c4 c4_var ln4_sq ln4_std elu_min elu_exp "
            "score_tables weights3 bases counted deg_row parts0 parts1 final").split()}

        block = ctx.enter_context(nc.Block())

        class Steps:

            def __init__(self, eng, s):
                self.eng, self.sem, self.n = eng, s, 0

            def __call__(self, ins):
                ins.then_inc(self.sem, 1)
                self.n += 1
                self.eng.wait_ge(self.sem, self.n)

        def take_flag(eng):
            eng.wait_ge(s_flag, 1)
            return eng.value_load(flag[0:1, 0:1], min_val=0, max_val=1)

        @block.sync
        def _(sp):
            sp.wait_ge(ready["pads_set"], 1)
            for n, a in enumerate((dst, src, et)):
                full = (G - 1) * RG * P
                sp.dma_start(rows_i[n][0:RG, 0:G - 1, :],
                             a[0:full].rearrange("(g p e) -> p g e", p=RG, e=P)).then_inc(s_rows, 16)
                last = full + (GL - 1) * P
                sp.dma_start(rows_i[n][0:GL - 1, G - 1, :],
                             a[full:last].rearrange("(p e) -> p e", e=P)).then_inc(s_rows, 16)
                sp.dma_start(rows_i[n][GL - 1:GL, G - 1, 0:TAIL],
                             a[last:E].rearrange("(p e) -> p e", p=1)).then_inc(s_rows, 16)
            sp.dma_start(X[:, 0:FULL, :], x[0:FULL * P, :].rearrange("(b p) d -> p b d", p=P)).then_inc(s_x, 16)
            sp.dma_start(X[0:REST, FULL, :], x[FULL * P:N, :]).then_inc(s_x, 16)
            loads = [
                (W0[:, :], w0), (B0[:, :], b0.rearrange("(p d) -> p d", p=1)),
                (WR[:, :, :], wrel.rearrange("r k d -> k r d")),
                (WSn[:, :], wself), (BS[:, :], bself.rearrange("(p d) -> p d", p=1)),
                (WLn[:, :], wlin), (WE[:, :], wedge),
            ]
            loads += [(att[:, n:n + 1], a[0, :, :].rearrange("h (c o) -> (h c) o", o=1))
                      for n, a in enumerate((attsrc, attdst, attedge))]
            loads += [(vecs[:, n, :], a.rearrange("(p d) -> p d", p=1).broadcast_to([P, D]))
                      for n, a in enumerate((bias, gamma, beta))]
            for o, i in loads:
                sp.dma_start(o, i).then_inc(s_w, 16)
            assert 16 * len(loads) == W_ALL
            sp.dma_start(base_row[0:1, 0:T // 2 - 1].unsqueeze(2),
                         dst[0:(T - 2) * P].rearrange("(o n e) -> o n e", o=1, e=2 * P)[:, :, 0:1],
                         allow_slow_non_contiguous=True).then_inc(s_base, 16)
            sp.dma_start(base_row[0:1, T // 2 - 1:T // 2],
                         dst[(T - 2) * P:(T - 2) * P + 1].rearrange("(o k) -> o k", o=1)).then_inc(s_base, 16)

            sp.wait_ge(ready["index_rows"], 1)
            for g in range(G):
                n = RG if g < G - 1 else GL
                sp.dma_start(block_lin[g * RG:g * RG + n, :], b0_lin[0:n, g, :]).then_inc(s_scr, 16)
            for row, b in ((src_lo_row, lo_b[0]), (dst_lo_row, lo_b[1])):
                sp.dma_start(row[0:(G - 1) * RG * P].rearrange("(g p e) -> p g e", p=RG, e=P),
                             b[0:RG, 0:G - 1, :]).then_inc(s_scr, 16)
                sp.dma_start(row[(G - 1) * RG * P:T * P].rearrange("(p e) -> p e", e=P),
                             b[0:GL, G - 1, :]).then_inc(s_scr, 16)
            sp.wait_ge(s_scr, 16 * (G + 4))
            sp.wait_ge(ready["pads_set"], 1)
            sp.dma_start(b0_row[0:1, :, 0:K, :].rearrange("o i k w -> o i (k w)"),
                         block_lin.rearrange("(o i k) w -> o i (k w)", o=1, k=K)).then_inc(s_b0, 16)

            def write_table(n, mark):
                sp.wait_ge(ready[mark], 1)
                sp.dma_start(tabs[n].rearrange("(b p) d -> p b d", p=P), agg[:, :, :]).then_inc(s_tabr, 16)

            def slow_table(n, mark, source):
                sp.wait_ge(ready[mark], 1)
                sp.dma_start(tabs[n].rearrange("(b p) d -> p b d", p=P), source[:, :, :]).then_inc(s_tabs, 16)

            fits = take_flag(sp)
            with sp.If(fits == 0):
                slow_table(0, "table0", agg)
                slow_table(1, "table1", Hn)

            t2 = tab2.rearrange("(b p r) d -> b p (r d)", p=P, r=R)
            with sp.Fori(0, NB // 2) as i:
                for s in range(2):
                    sp.wait_ge(s_of, OF["rel"] + 2 * i + s + 3)
                    sp.dma_start(t2[bass.ds(2 * i + s, 1), :, :].rearrange("o p n -> (o p) n"), t2_stage[:, s, :]).then_inc(s_t2[s], 16)
            def edge_chunk(i, s, tiles):
                sp.dma_start(ea_buf[:, s, 0:tiles, :],
                             ea[bass.ds(i * (K * P), tiles * P), :].rearrange("(k p) f -> p k f", p=P)
                             ).then_inc(s_ea[s], 16)
            with sp.Fori(0, IT // 2) as j:
                for s in range(2):
                    sp.wait_ge(s_eau, 2 * j + s + 1)
                    edge_chunk(2 * j + s, s, K)
            sp.wait_ge(s_eau, IT)
            edge_chunk(IT - 1, 0, K - 1)
            sp.dma_start(ea_buf[0:TAIL, 0, K - 1, :], ea[(T - 1) * P:E, :]).then_inc(s_ea[0], 16)

            sp.wait_ge(ready["table3"], 1)
            sp.dma_start(score_tab.rearrange("(b p) h -> p b h", p=P), ssrc[:, :, :]).then_inc(s_stab, 16)
            write_table(3, "table3")

            def lo_rows(i, s):
                for w, row in enumerate((src_lo_row, dst_lo_row)):
                    sp.dma_start(rows[:, w, s, :], row[bass.ds(i * (K * P), K * P)]
                                 .rearrange("(o n) -> o n", o=1).broadcast_to([P, K * P])).then_inc(s_row[s], 16)
            sp.wait_ge(ready["table3"], 1)
            with sp.Fori(0, IT // 2) as j:
                for s in range(2):
                    sp.wait_ge(s_rowu, 2 * j + s + 1)
                    lo_rows(2 * j + s, s)
            sp.wait_ge(s_rowu, IT)
            lo_rows(IT - 1, 0)

            sp.wait_ge(ready["dst_pads"], 1)
            for h in range(H):
                full = (IT - 1) * K * P
                sp.dma_start(dt_[h * K:(h + 1) * K, 0:(IT - 1) * P].bitcast(I32).rearrange("k (i e) -> k i e", e=P),
                             dst[0:full].rearrange("(i k e) -> k i e", k=K, e=P)).then_inc(s_dt, 16)
                sp.dma_start(dt_[h * K:h * K + K - 1, (IT - 1) * P:IT * P].bitcast(I32),
                             dst[full:full + (K - 1) * P].rearrange("(k e) -> k e", e=P)).then_inc(s_dt, 16)
                sp.dma_start(dt_[h * K + K - 1:(h + 1) * K, (IT - 1) * P:(IT - 1) * P + TAIL].bitcast(I32),
                             dst[full + (K - 1) * P:E].rearrange("(k e) -> k e", k=1)).then_inc(s_dt, 16)
            sp.wait_ge(ready["ends"], 1)
            for q in range(5):
                sp.dma_start(ends[q, :, :].rearrange("h (i k) -> i h k", k=K),
                             ends_t[:, q, :].rearrange("i (h k) -> i h k", k=K)).then_inc(s_ends, 16)
            sp.wait_ge(s_ends, 16 * 5)
            sp.dma_start(ch[:, 0:5, :], ends.rearrange("q h t -> h q t")).then_inc(s_ends, 16)
            sp.wait_ge(ready["carries"], 1)
            sp.dma_start(carries.rearrange("q h t -> h q t"), ch[:, 7:9, :]).then_inc(s_ends, 16)
            sp.wait_ge(s_ends, 16 * 7)
            for q in range(2):
                sp.dma_start(car_t[:, q, :].rearrange("i (h k) -> i h k", k=K),
                             carries[q, :, :].rearrange("h (i k) -> i h k", k=K)).then_inc(s_ends, 16)

            for n, b in enumerate(PARTS):
                sp.wait_ge(ready["final"], n + 1)
                end = min(b.stop, FULL)
                sp.dma_start(out[b.start * P:end * P, :].rearrange("(b p) d -> p b d", p=P), X[:, b.start:end, :]).then_inc(s_out, 16)
            sp.dma_start(out[FULL * P:N, :], X[0:REST, FULL, :]).then_inc(s_out, 16)
            sp.wait_ge(s_out, 16 * 3)

        @block.gpsimd
        def _(pool):
            pool.iota(io_p[:, :], [[0, 1]], base=0, channel_multiplier=1).then_inc(s_io, 1)
            pool.iota(io_w[:, :], [[1, 256]], base=0, channel_multiplier=0).then_inc(s_io, 1)
            pool.memset(ones[:, :], 1.0).then_inc(s_io, 1)
            pool.memset(zeros[:, :], 0.0).then_inc(s_io, 1)
            pool.memset(zero_w[:, :], 0.0).then_inc(s_io, 1)
            pool.iota(io_c[:, :], [[1, HI * W]], base=0, channel_multiplier=0).then_inc(s_io, 1)
            pool.memset(ones_b[:, :], 1.0).then_inc(s_io, 1)
            pool.wait_ge(ready["index_cols"], 1)
            pool.wait_ge(s_scr, 16 * (G + 4))
            pool.memset(count.rearrange("p b d -> p (b d)").bitcast(I32), 0).then_inc(s_cnt0, 1)

            pool.wait_ge(ready["h0"], 1)
            pool.sem_inc(s_so, 1)
            with pool.Fori(0, IT) as i:
                pool.wait_ge(s_so, len(BY_POOL) * i + 1)
                pool.tensor_copy(slo_buf[:, :], slo[:, bass.ds(i * K, K)]).then_inc(s_slo, 1)
                pool.wait_ge(s_slo, i + 1)
                pool.sem_inc(s_held, 1)
                for p in BY_POOL:
                    pool.wait_ge(s_pm, NP * i + p + 1)
                    pool.sem_inc(s_held, 1)
                    for k in (2 * p, 2 * p + 1):
                        last = pool.tensor_scalar(src_oh[:, k, :], wide_b[:, 0:P], slo_buf[:, k:k + 1], None, ALU.is_equal)
                    last.then_inc(s_so, 1)

            def gather(r, n, m, table, indices):
                with pool.Fori(0, IT) as i:
                    for half in range(2):
                        pool.wait_ge(r.mm, mm(n) + i * K + HK * (half + 1))
                        pool.sem_inc(s_held, 1)
                        pool.tensor_copy(idx_buf[:, half * HK:(half + 1) * HK],
                                         indices[:, bass.ds(i * K + half * HK, HK)]).then_inc(r.ix, 1)
                        pool.wait_ge(r.ix, 2 * IT * m + 2 * i + half + 1)
                        pool.sem_inc(s_held, 1)
                        for k in range(half * HK, (half + 1) * HK):
                            pool.indirect_dma_start(
                                out=xg[:, k, :], out_offset=None, in_=table,
                                in_offset=bass.IndirectOffsetOnAxis(ap=idx_buf[:, k:k + 1], axis=0)
                            ).then_inc(r.g[k // r.share], 16)

            fits = take_flag(pool)
            with pool.If(fits == 0):
                for n in range(2):
                    pool.wait_ge(s_tabs, 16 * (n + 1))
                    gather(slow, n + 1, n, tabs[n], idx)
            for t in s_t2:
                pool.wait_ge(t, 16 * (NB // 2))
            gather(main, 0, 0, tab2, hidx)
            pool.wait_ge(s_stab, 16)
            def gather_scores(i, s):
                pool.wait_ge(s_rq, NQ * (i + 1))
                pool.sem_inc(s_held, 1)
                pool.tensor_copy(sg_idx[:, s, :], idx[:, bass.ds(i * K + 4 * NM, K - 4 * NM)]).then_inc(s_sgi, 1)
                pool.wait_ge(s_sgi, i + 1)
                pool.sem_inc(s_held, 1)
                for k in range(K - 4 * NM):
                    pool.indirect_dma_start(
                        out=sg[:, s, k // 4, k % 4, :], out_offset=None, in_=score_tab,
                        in_offset=bass.IndirectOffsetOnAxis(ap=sg_idx[:, s, k:k + 1], axis=0)
                    ).then_inc(s_sg[s][k // 4], 16)
            with pool.Fori(0, IT // 2) as j:
                for s in range(2):
                    gather_scores(2 * j + s, s)
            gather_scores(IT - 1, 0)
            pool.wait_ge(s_tabr, 16)
            pool.wait_ge(ready["ring_free"], 1)
            gather(main, 1, 1, tab3, idx)

        @block.scalar
        def _(act):
            step = Steps(act, s_a)

            def mark(name):
                act.sem_inc(ready[name], 1)

            def std(v_mark, name):
                for n, b in enumerate(PARTS):
                    act.wait_ge(ready[v_mark], n + 1)
                    step(act.activation(sq[:, b, :], cen[:, b, :], ACT.Square))
                    mark(name + "_sq")
                for n, b in enumerate(PARTS):
                    act.wait_ge(ready[v_mark + "_var"], n + 1)
                    step(act.activation(st[:, 3, b], st[:, 2, b], ACT.Sqrt))
                    mark(name + "_std")

            def turn_blocks(n, source, mark_v, mm_used):
                act.wait_ge(ready[mark_v], 1)
                def pair(i, first=False):
                    for s in range(2):
                        act.activation(stage[:, s, :], source[:, bass.ds(2 * i + s, 1), :].rearrange("p o d -> p (o d)"), ACT.Copy).then_inc(s_st, 1)
                    for s in range(2):
                        act.wait_ge(s_tp, NB * n + 2 * i + s + 1)
                        act.wait_ge(s_of, mm_used + 2 * i + s + 1)
                        act.activation(lt[:, s, :], turned[s], ACT.Copy).then_inc(s_lt, 1)
                    if n == 0:
                        for s in range(2):
                            act.wait_ge(s_mo, 2 * i + s + 1)
                            act.activation(gl[:, s, :], ps[:, s * BK + D:s * BK + 2 * D], ACT.Gelu).then_inc(s_ae0, 1)
                    if n == 1:
                        for s in range(2):
                            act.wait_ge(s_mo, NB + 2 * i + s + 1)
                            if not first:
                                act.wait_ge(s_t2[s], 16 * i)
                            act.activation(t2_stage[:, s, 512:1024],
                                           ps[:, (3 * s + 1) * BK:(3 * s + 2) * BK], ACT.Copy).then_inc(s_ae, 1)
                pair(0, True)
                half = PARTS[0].stop // 2
                with act.Fori(1, half) as i:
                    pair(i)
                if n > 0:
                    act.wait_ge(ready[mark_v], 2)
                with act.Fori(half, NB // 2) as i:
                    pair(i)

            act.sem_inc(s_ztc, 2)
            def cast_slabs(n):
                with act.Fori(0, HI) as b:
                    act.wait_ge(s_su[0], n * HI + b + 1)
                    act.activation(slabs[0], count[:, bass.ds(b, 1), 0:SLAB[0]].rearrange("p o d -> p (o d)"),
                                   ACT.Copy).then_inc(s_sl[0], 1)

            std("c0", "ln0")
            act.wait_ge(ready["h0"], 1)
            act.wait_ge(ready["index_cols"], 1)
            act.sem_inc(s_ao, 1)
            with act.Fori(0, IT) as i:
                act.wait_ge(s_ao, len(BY_ACT) * i + 1)
                act.activation(slo_act, slo[:, bass.ds(i * K, K)], ACT.Copy).then_inc(s_sla, 1)
                act.wait_ge(s_sla, i + 1)
                for r, p in enumerate(BY_ACT):
                    act.wait_ge(s_pm, NP * i + p + 1)
                    for k in range(2):
                        act.activation(away[:, k, :], wide[:, 0:P], ACT.Abs, bias=slo_act[:, 2 * p + k:2 * p + k + 1],
                                       scale=-1.0).then_inc(s_away, 1)
                    for k in range(2):
                        act.wait_ge(s_away, 2 * len(BY_ACT) * i + 2 * r + k + 1)
                        last = act.activation(src_oh[:, 2 * p + k, :], away[:, k, :], ACT.Relu, bias=ones[:, 0:1], scale=-1.0)
                    last.then_inc(s_ao, 1)
                    if p != BY_ACT[-1]:
                        act.wait_ge(s_ao, len(BY_ACT) * i + r + 2)
            act.wait_ge(ready["counted"], 1)
            cast_slabs(0)
            act.wait_ge(ready["deg"], 1)
            step(act.activation(dinv[:, :], st[:, 4, :], ACT.Sqrt))
            mark("sqrt_deg")
            fits = take_flag(act)
            with act.If(fits > 0):
                act.wait_ge(ready["parts0"], 1)
                cast_slabs(1)
            turn_blocks(0, agg, "agg0", OF["gcn"])
            std("c1", "ln1")
            with act.If(fits > 0):
                act.wait_ge(ready["parts1"], 1)
                cast_slabs(2)
            std("c2", "ln2")
            turn_blocks(1, Hn, "h2", OF["rel"])
            std("c3", "ln3")
            turn_blocks(2, Hn, "h3", OF["att"])
            def out_z(i, s):
                act.wait_ge(s_zt, i + 1)
                act.activation(zt[0:RG, bass.ds(i * P, P)], ps[0:RG, s * BK:s * BK + P], ACT.Copy).then_inc(s_ztc, 1)

            def out_m(i, s):
                act.wait_ge(s_zt, IT + i + 1)
                act.activation(ZM[:, bass.ds(i, 1), :, :].rearrange("p o h k -> p (o h k)"),
                               ps[:, s * BK:s * BK + RG], ACT.Copy).then_inc(s_ztc, 1)
            for f in (out_z, out_m):
                with act.Fori(0, IT // 2) as j:
                    for s in range(2):
                        f(2 * j + s, s)
                f(IT - 1, 0)
            act.wait_ge(ready["alpha"], 1)
            for w in WEIGHTS:
                step(act.activation(eaf[:, w], eaf[:, w], ACT.Exp))
                mark("exp")
            def stage_weights(i):
                for half in range(2):
                    act.wait_ge(main.mm, mm(1) + i * K + HK * (half + 1))
                    act.activation(e_buf[:, half, :, :], EA[:, bass.ds(i, 1), :, half * HK:(half + 1) * HK]
                                   .rearrange("p o h k -> p (o k) h"), ACT.Copy)
                    for n in range(3):
                        last = act.activation(e3_buf[:, half, :, n * H:(n + 1) * H],
                                              E3[:, n, bass.ds(i * (H * K), H * K)].rearrange("p (h k) -> p k h", h=H)
                                              [:, half * HK:(half + 1) * HK, :], ACT.Copy)
                    last.then_inc(s_eb, 1)
            for n, steps in enumerate(((0, FIRST), (FIRST, IT))):
                act.wait_ge(ready["weights3"], n + 1)
                with act.Fori(*steps) as i:
                    stage_weights(i)
            std("c4", "ln4")
            for n, b in enumerate(PARTS):
                act.wait_ge(ready["elu_min"], n + 1)
                step(act.activation(sq[:, b, :], agg[:, b, :], ACT.Exp))
                mark("elu_exp")

        @block.vector
        def _(dve):
            step = Steps(dve, s_v)

            def mark(name):
                dve.sem_inc(ready[name], 1)

            def tt(o, a, b, op):
                step(dve.tensor_tensor(o, a, b, op))

            def ts(o, a, s1, s2, op0, op1=None):
                if op1 is None:
                    step(dve.tensor_scalar(o, a, s1, None, op0))
                else:
                    step(dve.tensor_scalar(o, a, s1, s2, op0, op1))

            def split3(parts, a, left):
                for n in range(3):
                    source = a if n == 0 else left
                    step(dve.tensor_copy(parts[:, n], source))
                    if n < 2:
                        tt(left, source, parts[:, n], ALU.subtract)

            def across(ap, n=D):
                return ap.unsqueeze(2).broadcast_to([ap.shape[0], ap.shape[1], n])

            def layernorm(name, mark_c, out, mark_out=None):
                source = X if name != "ln4" else agg
                for b in PARTS:
                    step(dve.tensor_reduce(st[:, 0, b], source[:, b, :], AX.X, ALU.add))
                    ts(st[:, 1, b], st[:, 0, b], 1.0 / D, None, ALU.mult)
                    tt(cen[:, b, :], source[:, b, :], across(st[:, 1, b]), ALU.subtract)
                    mark(mark_c)
                for n, b in enumerate(PARTS):
                    dve.wait_ge(ready[name + "_sq"], n + 1)
                    step(dve.tensor_reduce(st[:, 0, b], sq[:, b, :], AX.X, ALU.add))
                    ts(st[:, 2, b], st[:, 0, b], 1.0 / D, EPS, ALU.mult, ALU.add)
                    mark(mark_c + "_var")
                for n, b in enumerate(PARTS):
                    dve.wait_ge(ready[name + "_std"], n + 1)
                    step(dve.reciprocal(st[:, 5, b], st[:, 3, b]))
                    if name == "ln4":
                        tt(out[:, b, :], cen[:, b, :], across(st[:, 5, b]), ALU.mult)
                    else:
                        step(dve.scalar_tensor_tensor(out[:, b, :], cen[:, b, :], 0.0, across(st[:, 5, b]), ALU.max, ALU.mult))
                    if mark_out is not None:
                        mark(mark_out)

            dve.sem_inc(s_of, 2)
            dve.sem_inc(s_qd, 7)
            dve.sem_inc(s_pa, NP)
            dve.sem_inc(s_rq, 2 * NQ)
            dve.sem_inc(s_eau, 2)
            dve.sem_inc(s_rowu, 2)

            for n in range(3):
                step(dve.memset(rows_i[n][:, G - 1, :], 0 if n == 2 else PAD_NODE))
            step(dve.memset(X[:, FULL:NB, :], 0.0))
            step(dve.memset(b0_row[:, :, K:28, :], 0))
            mark("pads_set")
            step(dve.memset(head[:, :], 0.0))
            for h in range(H):
                step(dve.memset(head[h * C:(h + 1) * C, h:h + 1], 1.0))
            step(dve.memset(sdst[:, :, :], 0.0))
            dve.wait_ge(s_io, 7)
            step(dve.tensor_copy(wide_c[:, :], io_c[:, :]))
            step(dve.tensor_copy(part[:, :], io_p[:, :]))
            step(dve.tensor_copy(wide[:, :], io_w[:, :]))
            step(dve.tensor_copy(wide_b[:, :], io_w[:, :]))
            ts(ident[:, :], wide[:, 0:P], part[:, 0:1], None, ALU.is_equal)
            dve.wait_ge(s_rows, 16 * 9)
            di, si, ti = (r[0:RG, :, :] for r in rows_i)
            relf, srcf, hidf, hif, dstf = (r[0:RG, :, :] for r in rows_f)
            for w, e in ((0, 0), (1, P - 1)):
                step(dve.tensor_single_scalar(b0_lin[:, :, w:w + 1], di[:, :, e:e + 1], 7, ALU.arith_shift_right))
            tt(b0_lin[:, :, 1], b0_lin[:, :, 1], b0_lin[:, :, 0], ALU.subtract)
            step(dve.tensor_copy(b0_f[:, :], b0_lin[:, :, 0]))
            ts(b0_f[:, :], b0_f[:, :], float(P), None, ALU.mult)
            step(dve.tensor_copy(relf, di))
            step(dve.tensor_copy(dstf, di))
            tt(relf, relf, across(b0_f[:, :], P), ALU.subtract)
            step(dve.tensor_copy(srcf, si))
            step(dve.tensor_copy(hidf, ti))
            step(dve.scalar_tensor_tensor(hidf, srcf, float(R), hidf, ALU.mult, ALU.add))
            step(dve.tensor_single_scalar(lo_i[0:RG, :, :], si, P - 1, ALU.bitwise_and))
            step(dve.tensor_copy(lo_b[0][0:RG, :, :], lo_i[0:RG, :, :]))
            step(dve.tensor_copy(hif, lo_i[0:RG, :, :]))
            tt(hif, srcf, hif, ALU.subtract)
            ts(hif, hif, 1.0 / P, None, ALU.mult)
            step(dve.tensor_single_scalar(lo_i[0:RG, :, :], di, P - 1, ALU.bitwise_and))
            step(dve.tensor_copy(lo_b[1][0:RG, :, :], lo_i[0:RG, :, :]))
            mark("index_rows")
            for n, o in enumerate((rel, idx, hidx, hi, code)):
                for g in range(G):
                    m = RG if g < G - 1 else GL
                    c = n * G + g
                    dve.wait_ge(s_t, c + 1)
                    dve.tensor_copy(o[:, g * RG:g * RG + m], ps[:, (c % 8) * BK:(c % 8) * BK + m]).then_inc(s_tc, 1)
            dve.wait_ge(s_tc, 5 * G)
            step(dve.scalar_tensor_tensor(slo[:, :], hi[:, :], -float(P), idx[:, :], ALU.mult, ALU.add))
            dve.wait_ge(s_base, 32)
            step(dve.tensor_copy(base_f, base_row[:, :]))
            mark("bases")
            dve.wait_ge(s_bc, 1)
            c3 = code[:, :].rearrange("p (n w) -> p n w", w=2)
            tt(c3, c3, across(ps[:, 0:T // 2], 2), ALU.subtract)
            ts(inside[:, :], code[:, :], 0.0, None, ALU.is_ge)
            ts(in_tmp, code[:, :], float(W), None, ALU.is_lt)
            tt(inside[:, :], inside[:, :], in_tmp, ALU.mult)
            step(dve.scalar_tensor_tensor(code[:, :], hi[:, :], float(W), code[:, :], ALU.mult, ALU.add))
            step(dve.scalar_tensor_tensor(code[:, :], code[:, :], 1.0, inside[:, :], ALU.add, ALU.mult))
            ts(code[:, :], code[:, :], 1.0, None, ALU.subtract)
            mark("index_cols")
            dve.wait_ge(s_scr, 16 * (G + 4))

            dve.wait_ge(s_w, W_ALL)
            for n in range(3):
                ts(att3[:, n, :], head[:, :], att[:, n:n + 1], None, ALU.mult)
            for h in range(H):
                ts(att_wide[:, h, :], ones[:, :], att3[:, 2, h:h + 1], None, ALU.mult)
            mark("att")
            dve.wait_ge(s_pe0, 1)
            step(dve.tensor_copy(WS[:, :], ps[:, 0:D]))
            step(dve.tensor_copy(WL[:, 0:D], ps[:, BK:BK + D]))
            step(dve.tensor_copy(WL[:, D:D + 2 * H], ps[:, 2 * BK:2 * BK + 2 * H]))
            step(dve.tensor_copy(U[:, :, :], ps[:, 3 * BK:3 * BK + H * ED].rearrange("p (h f) -> p h f", f=ED)))
            mark("weights")

            dve.wait_ge(s_x, 32)
            layernorm("ln0", "c0", cen)
            mark("h0")

            def onehots(r, n, i, k):
                if k % HK == 0:
                    dve.wait_ge(r.mm, mm(n) + i * K + k + HK)
                dve.tensor_scalar(oh[:, k, :], wide[:, :], rel[:, bass.ds(i * K + k, 1)], None,
                                  ALU.is_equal).then_inc(r.oh, 1)

            def load_bases(i, p):
                n = min(4, NP - p)
                return nc.values_load_multi_w_load_instructions(
                    base_row[0:1, bass.ds(i * NP + p, n)],
                    engines=(DVE,), min_val=0, max_val=N - 1,
                    skip_runtime_bounds_check_because="destinations are nodes")[1]

            def pair_onehots(i, p):
                dve.wait_ge(s_pm, NP * i + p + 1)
                for k in (2 * p, 2 * p + 1):
                    last = dve.tensor_scalar(pair_oh[k % 2][:, p, :], wide_c[:, :], code[:, bass.ds(i * K + k, 1)], None,
                                             ALU.is_equal)
                last.then_inc(s_po, 1)

            def add_pair(i, p, regs):
                dve.wait_ge(s_pm, NP * i + p + 1 + NP)
                dve.wait_ge(s_pa, NP * i + p + NP)
                window = count[:, :, bass.ds(regs[p % 4], W)]
                dve.tensor_tensor(window, window, ps[:, (p % 8) * BK:(p % 8) * BK + HI * W].rearrange("p (b w) -> p b w", w=W),
                                  ALU.add).then_inc(s_pa, 1)

            dve.wait_ge(s_cnt0, 1)
            def pair_step(i, more=True):
                for p in range(NP):
                    if p + 2 < NP:
                        pair_onehots(i, p + 2)
                    elif more:
                        pair_onehots(i + 1, p + 2 - NP)
                    if p % 4 == 0:
                        regs = load_bases(i, p)
                    add_pair(i, p, regs)
            pair_onehots(0, 0)
            pair_onehots(0, 1)
            with dve.Fori(0, IT - 1) as i:
                pair_step(i)
            pair_step(IT - 1, more=False)
            dve.wait_ge(s_pa, NP + T // 2)
            mark("counted")

            def cast_slabs(n, done):
                with dve.Fori(0, HI) as b:
                    dve.wait_ge(s_su[1], n * HI + b + 1)
                    dve.tensor_copy(slabs[1], count[:, bass.ds(b, 1), SLAB[0]:BW].rearrange("p o d -> p (o d)")
                                    ).then_inc(s_sl[1], 1)
                dve.wait_ge(s_dense, done)

            cast_slabs(0, 1)
            step(dve.tensor_copy(deg_row, ps[0:1, 0:BW]))
            mark("deg_row")
            step(dve.tensor_reduce(total[:, :], deg_row, AX.X, ALU.add))
            step(dve.tensor_scalar(flag[:, :], total[:, :], float(E), None, ALU.is_equal))
            dve.wait_ge(s_tot, 1)
            step(dve.tensor_copy(deg[:, :], small[:, 0:NB]))
            dve.sem_inc(s_flag, 1)
            fits = take_flag(dve)
            with dve.If(fits == 0):
                with dve.Fori(0, IT) as i:
                    for k in range(K):
                        onehots(slow, 0, i, k)
                dve.wait_ge(slow.mm, K + mm(1))
                dve.tensor_copy(deg[:, :], small[:, 0:NB]).then_inc(s_sv, 1)
                dve.wait_ge(s_sv, 1)
            ts(st[:, 4, :], deg[:, :], 1.0, None, ALU.add)
            mark("deg")
            ts(deg[:, :], deg[:, :], 1.0, None, ALU.max)
            step(dve.reciprocal(rdeg[:, :], deg[:, :]))
            dve.wait_ge(ready["sqrt_deg"], 1)
            step(dve.reciprocal(dinv[:, :], dinv[:, :]))
            tt(agg, cen, across(dinv[:, :]), ALU.mult)
            mark("table0")

            def sum_neighbours(n, table):
                with dve.If(fits > 0):
                    c = 0
                    for half in range(2):
                        cols = slice(half * NPAD // 2, (half + 1) * NPAD // 2)
                        for m in range(3):
                            source = table[:, cols] if m == 0 else left
                            dve.tensor_copy(parts[:, m, cols], source).then_inc(s_split[n], 1)
                            dve.wait_ge(s_split[n], c + 1)
                            c += 1
                            if m < 2:
                                dve.tensor_tensor(left, source, parts[:, m, cols], ALU.subtract).then_inc(s_split[n], 1)
                                dve.wait_ge(s_split[n], c + 1)
                                c += 1
                    dve.sem_inc(ready[f"parts{n}"], 2)
                    cast_slabs(n + 1, n + 2)
                with dve.If(fits == 0):
                    with dve.Fori(0, IT) as i:
                        for k in range(K):
                            onehots(slow, n + 1, i, k)
                    dve.wait_ge(slow.mm, K + mm(n + 2))

            sum_neighbours(0, agg.rearrange("p b d -> p (b d)"))
            tt(agg, acc[:, 0:NPAD].rearrange("p (b d) -> p b d", d=D), agg, ALU.add)
            tt(agg, agg, across(dinv[:, :]), ALU.mult)
            mark("agg0")

            def edge_term(i, s):
                for h in range(H):
                    c = 2 * h
                    dve.tensor_tensor(ea_tmp, ea_buf[:, s, :, :],
                                      U[:, h, :].unsqueeze(1).broadcast_to([P, K, ED]), ALU.mult).then_inc(s_et, 1)
                    dve.wait_ge(s_et, 8 * i + c + 1)
                    dve.tensor_reduce(EA[:, bass.ds(i, 1), h, :].rearrange("p o k -> p (o k)"), ea_tmp, AX.X, ALU.add).then_inc(s_et, 1)
                    dve.wait_ge(s_et, 8 * i + c + 2)
                dve.sem_inc(s_eau, 1)

            def take_sums(factor):
                tt(agg, acc[:, 0:NPAD].rearrange("p (b d) -> p b d", d=D), across(factor), ALU.mult)

            with dve.Fori(0, NB // 2) as i:
                for s in range(2):
                    dve.wait_ge(s_ae0, 2 * i + s + 1)
                    dve.tensor_tensor(ab[:, s, :], ps[:, s * BK:s * BK + D], gl[:, s, :], ALU.mult).then_inc(s_of, 1)
                    dve.wait_ge(s_of, OF["gcn"] + 2 * i + s + 3)
                    xb = X[:, bass.ds(2 * i + s, 1), :].rearrange("p o d -> p (o d)")
                    dve.tensor_tensor(xb, xb, ab[:, s, :], ALU.add).then_inc(s_xb, 1)
            dve.wait_ge(s_xb, NB)

            layernorm("ln1", "c1", Hn)
            mark("table1")
            sum_neighbours(1, Hn[:, :, :].rearrange("p b d -> p (b d)"))
            take_sums(rdeg[:, :])
            step(dve.scalar_tensor_tensor(agg, agg, 0.5, Hn[:, :, :], ALU.mult, ALU.add))
            tt(X[:, :, :], X[:, :, :], agg, ALU.add)

            layernorm("ln2", "c2", Hn, "h2")
            def take_relations(i, first=False):
                for s in range(2):
                    dve.wait_ge(s_mo, NB + 2 * i + s + 1)
                    if not first:
                        dve.wait_ge(s_t2[s], 16 * i)
                    dve.tensor_copy(cen[:, bass.ds(2 * i + s, 1), :].rearrange("p o d -> p (o d)"),
                                    ps[:, (3 * s + 2) * BK:(3 * s + 2) * BK + D]).then_inc(s_xb, 1)
                    dve.tensor_copy(t2_stage[:, s, 0:512], ps[:, 3 * s * BK:(3 * s + 1) * BK]).then_inc(s_xb, 1)
                    dve.wait_ge(s_xb, NB + 4 * i + 2 * s + 2)
                    dve.wait_ge(s_ae, 2 * i + s + 1)
                    dve.sem_inc(s_of, 1)
            take_relations(0, True)
            with dve.Fori(1, NB // 2) as i:
                take_relations(i)
            with dve.Fori(0, IT // 2) as j:
                for s in range(2):
                    for k in range(K):
                        onehots(main, 0, 2 * j + s, k)
                    dve.wait_ge(s_ea[s], 16 * j + 16)
                    edge_term(2 * j + s, s)
            for k in range(K):
                onehots(main, 0, IT - 1, k)
            dve.wait_ge(s_ea[0], 16 * (IT // 2) + 32)
            edge_term(IT - 1, 0)

            dve.wait_ge(main.mm, K + mm(1))
            take_sums(rdeg[:, :])
            tt(agg, agg, cen, ALU.add)
            step(dve.scalar_tensor_tensor(X[:, :, :], agg, 0.0, X[:, :, :], ALU.max, ALU.add))

            layernorm("ln3", "c3", Hn, "h3")
            with dve.Fori(0, NB // 2) as i:
                for s in range(2):
                    b = bass.ds(2 * i + s, 1)
                    dve.wait_ge(s_mo, 2 * NB + 2 * i + s + 1)
                    o = ps[:, s * BK:s * BK + D + 2 * H]
                    dve.tensor_copy(agg[:, b, :].rearrange("p o d -> p (o d)"), o[:, 0:D]).then_inc(s_xb, 1)
                    dve.tensor_copy(sdst[:, b, :].rearrange("p o d -> p (o d)"), o[:, D:D + H]).then_inc(s_xb, 1)
                    dve.tensor_copy(ssrc[:, b, :].rearrange("p o d -> p (o d)"), o[:, D + H:D + 2 * H]).then_inc(s_xb, 1)
                    dve.wait_ge(s_xb, 3 * NB + 6 * i + 3 * s + 3)
                    dve.sem_inc(s_of, 1)
            dve.wait_ge(s_of, OF["end"] + 2)
            mark("table3")
            split3(ssrc3, ssrc[:, :, :].rearrange("p b h -> p (b h)"), split_tmp[:, 0:NB * H])
            split3(sdst3[:, :, :, :].rearrange("p b n h -> p n b h"), sdst[:, :, :], split_tmp[:, :].rearrange("p (b h) -> p b h", h=H))
            ts(bh_row, b0_row[:, :, :, 0], float(3 * H), None, ALU.mult)
            mark("score_tables")

            def build(i, q, s):
                n = 4 if q < NQ - 1 else 2
                cols = slice(q * 4 * P, q * 4 * P + n * P)
                for o, w in ((ohs, 0), (ohd, 1)):
                    if w == 0 and q >= NM:
                        continue
                    ins = dve.tensor_scalar(o[:, q, 0:n * P], rows[:, w, s, cols], part[:, 0:1], None, ALU.is_equal)
                ins.then_inc(s_qoh, 1)

            def pick(i, q, s, j):
                n = 4 if q < NQ - 1 else 2
                dve.wait_ge(s_qmm, NQ * i + q + 1)
                bank = ps[:, q * BK:(q + 1) * BK]
                if q < NM:
                    pr = prod[:, q % 2, :].rearrange("p (k b h) -> p k b h", b=NB, h=H)
                    dve.tensor_tensor(pr, bank[:, 0:4 * NB * H].rearrange("p (k b h) -> p k b h", b=NB, h=H),
                                      hi_mask[:, s, 4 * q:4 * q + 4, :].unsqueeze(3).broadcast_to([P, 4, NB, H]),
                                      ALU.mult).then_inc(s_prod, 1)
                dve.tensor_reduce(sd_two[:, s, 4 * q:4 * q + n, :].rearrange("p k (w h) -> p (k w) h", w=2),
                                  bank[:, 4 * NB * H:4 * NB * H + n * 6 * H].rearrange("p (x n h) -> p x h n", n=3, h=H),
                                  AX.X, ALU.add).then_inc(s_qd, 1)
                scores = ZM[:, bass.ds(i, 1), :, 4 * q:4 * q + n].rearrange("p o h k -> p (o k) h")
                if q < NM:
                    dve.wait_ge(s_prod, NM * i + q + 1)
                    dve.tensor_reduce(scores, pr.rearrange("p k b h -> p k h b"), AX.X, ALU.add).then_inc(s_rq, 1)
                else:
                    dve.wait_ge(s_sg[s][q - NM], 16 * n * (j + 1))
                    dve.tensor_copy(scores, sg[:, s, q - NM, 0:n, :]).then_inc(s_rq, 1)

            def pass_a_step(i, s, j, more=True):
                dve.tensor_tensor(hi_mask[:, s, :, :],
                                  hi[:, bass.ds(i * K, 4 * NM)].unsqueeze(2).broadcast_to([P, 4 * NM, NB]),
                                  wide[:, 0:NB].unsqueeze(1).broadcast_to([P, 4 * NM, NB]), ALU.is_equal).then_inc(s_hm, 1)
                dve.tensor_scalar(in_block[:, s, 0, :], rel[:, bass.ds(i * K, K)], float(P), None, ALU.is_lt).then_inc(s_hm, 1)
                dve.tensor_scalar(in_block[:, s, 1, :], rel[:, bass.ds(i * K, K)], float(P), None, ALU.is_ge).then_inc(s_hm, 1)
                if more:
                    dve.wait_ge(s_row[1 - s], 32 * (j + s) + 32)
                dve.wait_ge(s_hm, 3 * i + 3)
                for q in range(NQ):
                    pick(i, q, s, j)
                    if more:
                        build(i + 1, q, 1 - s)
                dve.wait_ge(s_qd, NQ * (i + 2))
                two = sd_two[:, s, :, :].rearrange("p k (w h) -> p w h k", w=2)
                for w in range(2):
                    dve.tensor_tensor(two[:, w], two[:, w],
                                      in_block[:, s, w, :].unsqueeze(1).broadcast_to([P, H, K]), ALU.mult).then_inc(s_pr, 1)
                if more:
                    dve.wait_ge(s_qoh, NQ * (i + 2))
                    dve.sem_inc(s_rowu, 1)
                dve.wait_ge(s_pr, 3 * i + 2)
                dve.tensor_tensor(SD[:, bass.ds(i, 1), :, :].rearrange("p o h k -> p (o h) k"),
                                  two[:, 0], two[:, 1], ALU.add).then_inc(s_pr, 1)

            dve.wait_ge(s_row[0], 32)
            for q in range(NQ):
                build(0, q, 0)
            dve.wait_ge(s_qoh, NQ)
            dve.sem_inc(s_rowu, 1)
            with dve.Fori(0, IT // 2) as j:
                for s in range(2):
                    pass_a_step(2 * j + s, s, j)
            pass_a_step(IT - 1, 0, IT // 2, more=False)
            dve.wait_ge(s_pr, 3 * IT)
            dve.wait_ge(s_rq, 2 * NQ + NQ * IT)
            dve.wait_ge(s_tabr, 16)
            tt(EA[:, :, :, :], EA[:, :, :, :], ZM[:, :, :, :], ALU.add)
            step(dve.memset(dt_.bitcast(I32)[0:RG, (IT - 1) * P:IT * P], PAD_NODE))
            mark("dst_pads")

            def from_scores(i, s):
                return dve.tensor_copy(stage[:, s, 0:RG], EA[:, bass.ds(i, 1), :, :].rearrange("p o h k -> p (o h k)"))

            def from_maxima(i, s):
                return dve.tensor_copy(stage[0:RG, s, :], bw[0:RG, bass.ds(i * P, P)])

            def stage_all(copy, base):
                for s in range(2):
                    copy(s, s).then_inc(s_zs, 1)
                with dve.Fori(1, IT // 2) as j:
                    for s in range(2):
                        dve.wait_ge(s_zt, base + 2 * j + s - 1)
                        copy(2 * j + s, s).then_inc(s_zs, 1)
                dve.wait_ge(s_zt, base + IT - 2)
                copy(IT - 1, 0).then_inc(s_zs, 1)

            stage_all(from_scores, 0)
            dve.wait_ge(s_ztc, 2 + IT)
            dve.wait_ge(s_dt, 16 * 3 * H)
            d3 = dt_[0:RG, :].rearrange("r (i e) -> r i e", e=P)
            b3 = brk[0:RG, :].rearrange("r (i e) -> r i e", e=P)
            f3 = fw[0:RG, :].rearrange("r (i e) -> r i e", e=P)
            w3 = bw[0:RG, :].rearrange("r (i e) -> r i e", e=P)
            step(dve.tensor_copy(fw[0:RG, :], dt_[0:RG, :].bitcast(I32)))
            ts(dt_[0:RG, :], fw[0:RG, :], APART, None, ALU.mult)
            step(dve.memset(b3[:, :, 0:1], -BIG))
            tt(b3[:, :, 1:P], d3[:, :, 0:P - 1], d3[:, :, 1:P], ALU.subtract)
            step(dve.tensor_tensor_scan(fw[0:RG, :], brk[0:RG, :], zt[0:RG, :], -BIG, ALU.add, ALU.max))
            step(dve.memset(b3[:, :, P - 1:P], -BIG))
            tt(b3[:, :, 0:P - 1], d3[:, :, 0:P - 1], d3[:, :, 1:P], ALU.subtract)
            step(dve.tensor_tensor_scan(bw[0:RG, ::-1], brk[0:RG, ::-1], zt[0:RG, ::-1], -BIG, ALU.add, ALU.max))
            step(dve.tensor_copy(ends_sb[:, 0, :].unsqueeze(2), f3[:, :, P - 1:P]))
            step(dve.tensor_copy(ends_sb[:, 1, :].unsqueeze(2), w3[:, :, 0:1]))
            tt(ends_sb[:, 2, :].unsqueeze(2), d3[:, :, 0:1], d3[:, :, P - 1:P], ALU.is_equal)
            step(dve.tensor_copy(ends_sb[:, 3, :].unsqueeze(2), d3[:, :, 0:1]))
            step(dve.tensor_copy(ends_sb[:, 4, :].unsqueeze(2), d3[:, :, P - 1:P]))
            mark("ends_cols")
            dve.wait_ge(s_ect, 1)
            for q in range(5):
                step(dve.tensor_copy(ends_t[:, q, :], ps[0:IT, q * BK:q * BK + RG]))
            mark("ends")
            tt(EA[:, :, :, :], EA[:, :, :, :], SD[:, :, :, :], ALU.add)
            dve.wait_ge(s_ends, 16 * 6)
            step(dve.memset(ch[:, 5, 0:1], 0.0))
            tt(ch[:, 5, 1:T], ch[:, 3, 1:T], ch[:, 4, 0:T - 1], ALU.is_equal)
            tt(ch[:, 6, :], ch[:, 5, :], ch[:, 2, :], ALU.mult)
            ts(ch[:, 6, :], ch[:, 6, :], 1.0, BIG, ALU.subtract, ALU.mult)
            step(dve.tensor_tensor_scan(ch[:, 0, :], ch[:, 6, :], ch[:, 0, :], -BIG, ALU.add, ALU.max))
            step(dve.memset(ch[:, 6, T - 1:T], -BIG))
            tt(ch[:, 6, 0:T - 1], ch[:, 5, 1:T], ch[:, 2, 0:T - 1], ALU.mult)
            ts(ch[:, 6, 0:T - 1], ch[:, 6, 0:T - 1], 1.0, BIG, ALU.subtract, ALU.mult)
            step(dve.tensor_tensor_scan(ch[:, 1, ::-1], ch[:, 6, ::-1], ch[:, 1, ::-1], -BIG, ALU.add, ALU.max))
            ts(ch[:, 5, :], ch[:, 5, :], 1.0, BIG, ALU.subtract, ALU.mult)
            step(dve.memset(ch[:, 7, 0:1], -BIG))
            tt(ch[:, 7, 1:T], ch[:, 0, 0:T - 1], ch[:, 5, 1:T], ALU.add)
            step(dve.memset(ch[:, 8, T - 1:T], -BIG))
            tt(ch[:, 8, 0:T - 1], ch[:, 1, 1:T], ch[:, 5, 1:T], ALU.add)
            mark("carries")
            step(dve.scalar_tensor_tensor(eaf, eaf, 0.2, eaf, ALU.mult, ALU.max))
            dve.wait_ge(s_ends, 16 * 9)
            mark("carries_read")
            dve.wait_ge(s_ect, 2)
            for q in range(2):
                step(dve.tensor_copy(car_in[:, q, :], ps[0:RG, q * BK:q * BK + IT]))
            for q, o, c in ((0, f3, 3), (1, w3, 4)):
                end = across(ends_sb[:, c, :], P)
                tt(b3, *((end, d3) if q == 0 else (d3, end)), ALU.subtract)
                tt(b3, b3, across(car_in[:, q, :], P), ALU.add)
                tt(o, o, b3, ALU.max)
            mark("ring_free")
            tt(w3, w3, f3, ALU.max)
            stage_all(from_maxima, IT)
            dve.wait_ge(s_ztc, 2 + 2 * IT)

            tt(ZM[:, :, :, :], ZM[:, :, :, :], SD[:, :, :, :], ALU.add)
            step(dve.scalar_tensor_tensor(zmf, zmf, 0.2, zmf, ALU.mult, ALU.max))
            tt(EA[:, :, :, :], EA[:, :, :, :], ZM[:, :, :, :], ALU.subtract)
            mark("alpha")
            def weigh_rows(i):
                for k in range(K):
                    onehots(main, 1, i, k)
                    dve.tensor_scalar(oh_b[:, k, :], wide_b[:, :], rel[:, bass.ds(i * K + k, 1)], None, ALU.is_equal)
                    if k % HK == 0:
                        dve.wait_ge(s_eb, 2 * i + k // HK + 1)
                    main.wait_gathered(dve, k, 1, i)
                    dve.tensor_tensor(xw[:, k, :].rearrange("p (h c) -> p h c", c=C),
                                      xg[:, k, :].rearrange("p (h c) -> p h c", c=C),
                                      e_buf[:, k // HK, k % HK, :].unsqueeze(2).broadcast_to([P, H, C]),
                                      ALU.mult).then_inc(s_xw, 1)
            for n, steps in enumerate(((0, FIRST), (FIRST, IT))):
                w = WEIGHTS[n]
                dve.wait_ge(ready["exp"], n + 1)
                split3(E3[:, :, w], eaf[:, w], cen.rearrange("p b d -> p (b d)")[:, w])
                mark("weights3")
                with dve.Fori(*steps) as i:
                    weigh_rows(i)
            dve.wait_ge(main.mm, K + mm(2))
            den3 = small[:, 0:NB * 3 * H].rearrange("p (b n h) -> p b h n", n=3, h=H)
            step(dve.tensor_reduce(den[:, :, :], den3, AX.X, ALU.add))
            ts(den[:, :, :], den[:, :, :], 1e-16, None, ALU.add)
            step(dve.reciprocal(rden[:, :, :], den[:, :, :]))
            tt(agg.rearrange("p b (h c) -> p (b h) c", c=C), acc[:, 0:NPAD].rearrange("p (n c) -> p n c", c=C),
               rden[:, :, :].rearrange("p b h -> p (b h)").unsqueeze(2).broadcast_to([P, NB * H, C]), ALU.mult)

            def over_blocks(n):
                return vecs[:, n, :].unsqueeze(1).broadcast_to([P, NB, D])
            tt(agg, agg, over_blocks(0), ALU.add)
            tt(agg, agg, Hn[:, :, :], ALU.add)
            layernorm("ln4", "c4", cen)
            for b in PARTS:
                def over_part(n):
                    return vecs[:, n, :].unsqueeze(1).broadcast_to([P, b.stop - b.start, D])
                tt(cen[:, b, :], cen[:, b, :], over_part(1), ALU.mult)
                tt(cen[:, b, :], cen[:, b, :], over_part(2), ALU.add)
                ts(agg[:, b, :], cen[:, b, :], 0.0, None, ALU.min)
                mark("elu_min")
            for n, b in enumerate(PARTS):
                dve.wait_ge(ready["elu_exp"], n + 1)
                step(dve.scalar_tensor_tensor(cen[:, b, :], cen[:, b, :], 0.0, X[:, b, :], ALU.max, ALU.add))
                step(dve.scalar_tensor_tensor(X[:, b, :], sq[:, b, :], -1.0, cen[:, b, :], ALU.add, ALU.add))
                mark("final")

        @block.tensor
        def _(pe):
            for r in (slow, main):
                pe.sem_inc(r.mm, K)
            pe.sem_inc(s_pm, NP)
            for n in range(2):
                pe.sem_inc(s_su[n], 1)

            pe.wait_ge(ready["index_rows"], 1)
            for n, r in enumerate(rows_f):
                for g in range(G):
                    m = RG if g < G - 1 else GL
                    c = n * G + g
                    if c >= 8:
                        pe.wait_ge(s_tc, c - 7)
                    pe.transpose(ps[:, (c % 8) * BK:(c % 8) * BK + m], r[0:m, g, :], ident[0:m, 0:m]).then_inc(s_t, 1)

            pe.wait_ge(ready["bases"], 1)
            pe.matmul(ps[:, 0:T // 2], ones[0:1, :], base_f, start=True, stop=True).then_inc(s_bc, 1)

            pe.wait_ge(ready["att"], 1)
            pe.transpose(ps[:, 0:D], WSn[:, :], ident[:, :])
            pe.transpose(ps[:, BK:BK + D], WLn[:, :], ident[:, :])
            pe.matmul(ps[:, 2 * BK:2 * BK + 2 * H], WLn[:, :], att3[:, 0:2, :].rearrange("p n h -> p (n h)"), start=True, stop=True)
            for h in range(H):
                last = pe.matmul(ps[:, 3 * BK + h * ED:3 * BK + (h + 1) * ED], att_wide[:, h, :], WE[:, :], start=True, stop=True)
            last.then_inc(s_pe0, 1)
            pe.wait_ge(ready["weights"], 1)
            pe.wait_ge(s_b0, 16)

            def load_blocks(i, k):
                return nc.values_load_multi_w_load_instructions(
                    b0_row[0:1, bass.ds(i, 1), k:k + 4, :].rearrange("p o k w -> p (o k w)"),
                    engines=(PE,), min_val=0, max_val=NB - 2,
                    skip_runtime_bounds_check_because="blocks are below NB - 1")[1]

            def zero_psum():
                for b in range(8):
                    last = pe.matmul(ps[:, b * BK:(b + 1) * BK], zero_w[:, :], zeros[:, :], start=True, stop=True)

            def add_block(k, b, w, kind):
                one = oh[:, k, w * P:(w + 1) * P]
                if kind == "count":
                    return pe.matmul(small[:, bass.ds(b + w, 1)], one, ones[:, 0:1],
                                     start=False, stop=False, skip_group_check=True)
                last = pe.matmul(acc[:, bass.ds(b * P + w * P, P)], one, (xw if kind == "weighted" else xg)[:, k, :],
                                 start=False, stop=False, skip_group_check=True)
                if kind == "weighted":
                    last = pe.matmul(small[:, bass.ds(b * (3 * H) + w * (3 * H), 3 * H)],
                                     oh_b[:, k, w * P:(w + 1) * P], e3_buf[:, k // HK, k % HK, :],
                                     start=False, stop=False, skip_group_check=True)
                return last

            def add_tiles(r, n, m, kind):
                zero_psum()
                with pe.Fori(0, IT) as i:
                    for k in range(K):
                        if k % 4 == 0:
                            regs = load_blocks(i, k)
                        b, reaches = regs[2 * (k % 4):2 * (k % 4) + 2]
                        if kind == "weighted":
                            pe.wait_ge(s_xw, i * K + k + 1)
                        else:
                            pe.wait_ge(r.oh, mm(n) + i * K + k + 1)
                            if kind == "rows":
                                r.wait_gathered(pe, k, m, i)
                        if kind == "weighted":
                            with pe.If(reaches > 0):
                                add_block(k, b, 1, kind)
                        else:
                            add_block(k, b, 1, kind)
                        last = add_block(k, b, 0, kind)
                        last.then_inc(r.mm, 1)

            def with_counts(n, product):
                zero_psum()
                with pe.Fori(0, HI) as b:
                    row = nc.tensor.snap(b * P)
                    for h in range(2):
                        pe.wait_ge(s_sl[h], n * HI + b + 1)
                        last = product(h, row)
                        last.then_inc(s_su[h], 1)

            def degrees(h, row):
                for c in range(0, SLAB[h], BK):
                    n = min(BK, SLAB[h] - c)
                    o = h * SLAB[0] + c
                    last = pe.matmul(ps[0:1, o:o + n], ones_b[:, :], slabs[h][:, c:c + n], start=False, stop=False,
                                     skip_group_check=True)
                return last

            def sums(h, row):
                for c in range(0, SLAB[h], P):
                    o = h * SLAB[0] + c
                    for m in range(3):
                        last = pe.matmul(acc[:, o:o + P], slabs[h][:, c:c + P], parts[:, m, bass.ds(row, P)],
                                         start=False, stop=False, skip_group_check=True)
                return last

            def sum_neighbours(n):
                with pe.If(fits > 0):
                    pe.wait_ge(ready[f"parts{n}"], 1)
                    with_counts(n + 1, sums)
                    pe.drain().then_inc(s_dense, 1)
                with pe.If(fits == 0):
                    add_tiles(slow, n + 1, n, "rows")

            def multiply_blocks(n, bank_of, product):
                with pe.Fori(0, NB // 2) as i:
                    for s in range(2):
                        pe.wait_ge(s_st, NB * n + 2 * i + s + 1)
                        pe.transpose(turned[s], stage[:, s, :], ident[:, :]).then_inc(s_tp, 1)
                    for s in range(2):
                        pe.wait_ge(s_lt, NB * n + 2 * i + s + 1)
                        pe.wait_ge(s_of, NB * n + 2 * i + s + 1)
                        product(s, bank_of * s * BK).then_inc(s_mo, 1)

            def gcn(s, o):
                pe.matmul(ps[:, o:o + 2 * D], ones[0:1, :], B0[:, :], start=True, stop=False)
                return pe.matmul(ps[:, o:o + 2 * D], lt[:, s, :], W0[:, :], start=False, stop=True)

            def relations(s, o):
                for c in range(2):
                    pe.matmul(ps[:, o + c * BK:o + (c + 1) * BK], lt[:, s, :],
                              WR[:, 4 * c:4 * c + 4, :].rearrange("p r d -> p (r d)"), start=True, stop=True)
                pe.matmul(ps[:, o + 2 * BK:o + 2 * BK + D], ones[0:1, :], BS[:, :], start=True, stop=False)
                return pe.matmul(ps[:, o + 2 * BK:o + 2 * BK + D], lt[:, s, :], WS[:, :], start=False, stop=True)

            def attention(s, o):
                return pe.matmul(ps[:, o:o + D + 2 * H], lt[:, s, :], WL[:, :], start=True, stop=True)

            with pe.Fori(0, IT) as i:
                for p in range(NP):
                    if p in BY_POOL:
                        pe.wait_ge(s_so, len(BY_POOL) * i + BY_POOL.index(p) + 2)
                    else:
                        pe.wait_ge(s_ao, len(BY_ACT) * i + BY_ACT.index(p) + 2)
                    pe.wait_ge(s_po, NP * i + p + 1)
                    free = NP * i + p + 1 + (8 if p < NP - 8 else 0 if p < 8 else NP - 8)
                    pe.wait_ge(s_pa, free)
                    for k in range(2):
                        last = pe.matmul(ps[:, (p % 8) * BK:(p % 8) * BK + HI * W], src_oh[:, 2 * p + k, :],
                                         pair_oh[k][:, p, :], start=(k == 0), stop=(k == 1))
                    last.then_inc(s_pm, 1)
            pe.wait_ge(ready["counted"], 1)
            with_counts(0, degrees)
            pe.drain().then_inc(s_dense, 1)
            pe.wait_ge(ready["deg_row"], 1)
            for b in range(HI):
                last = pe.matmul(small[:, b:b + 1], deg_row[:, b * P:(b + 1) * P], ones[0:1, 0:1],
                                 start=False, stop=False, skip_group_check=True)
            last.then_inc(s_tot, 1)
            fits = take_flag(pe)
            with pe.If(fits == 0):
                add_tiles(slow, 0, 0, "count")
            pe.wait_ge(ready["table0"], 1)
            sum_neighbours(0)
            multiply_blocks(0, 1, gcn)
            pe.wait_ge(ready["table1"], 1)
            sum_neighbours(1)
            pe.wait_ge(ready["h2"], 1)
            multiply_blocks(1, 3, relations)
            pe.wait_ge(s_of, OF["att"] + 2)
            add_tiles(main, 0, 0, "rows")
            pe.wait_ge(ready["h3"], 1)
            multiply_blocks(2, 1, attention)

            sdst3_rows = sdst3[:, :, :, :].rearrange("p b n h -> p (b n h)")
            pe.wait_ge(ready["score_tables"], 1)
            pe.wait_ge(s_of, OF["end"] + 2)

            with pe.Fori(0, IT) as i:
                for q in range(NQ):
                    n = 4 if q < NQ - 1 else 2
                    columns = nc.values_load_multi_w_load_instructions(
                        bh_row[0:1, bass.ds(i, 1), 4 * q:4 * q + n].rearrange("p o k -> p (o k)"),
                        engines=(PE,), min_val=0, max_val=(NB - 2) * 3 * H,
                        skip_runtime_bounds_check_because="blocks are below NB - 1")[1]
                    pe.wait_ge(s_qoh, NQ * i + q + 1)
                    pe.wait_ge(s_qd, NQ * i + q + 1)
                    for kk in range(n):
                        o = q * BK + kk * NB * H
                        for part3 in range(3 if q < NM else 0):
                            pe.matmul(ps[:, o:o + NB * H], ohs[:, q, kk * P:(kk + 1) * P], ssrc3[:, part3, :],
                                      start=(part3 == 0), stop=(part3 == 2))
                        o = q * BK + 4 * NB * H + kk * 6 * H
                        last = pe.matmul(ps[:, o:o + 6 * H], ohd[:, q, kk * P:(kk + 1) * P],
                                         sdst3_rows[:, bass.ds(columns[kk], 6 * H)], start=True, stop=True)
                    last.then_inc(s_qmm, 1)

            def turn(base, cols):
                def one(i, s):
                    pe.wait_ge(s_zs, base + i + 1)
                    pe.wait_ge(s_ztc, base + i + 1)
                    if cols:
                        pe.transpose(ps[0:RG, s * BK:s * BK + P], stage[:, s, 0:RG], ident[:, :]).then_inc(s_zt, 1)
                    else:
                        pe.transpose(ps[:, s * BK:s * BK + RG], stage[0:RG, s, :], ident[0:RG, 0:RG]).then_inc(s_zt, 1)
                with pe.Fori(0, IT // 2) as j:
                    for s in range(2):
                        one(2 * j + s, s)
                one(IT - 1, 0)

            pe.wait_ge(s_qd, NQ + NQ * IT)
            turn(0, True)
            pe.wait_ge(ready["ends_cols"], 1)
            for q in range(5):
                last = pe.transpose(ps[0:IT, q * BK:q * BK + RG], ends_sb[:, q, :], ident[0:RG, 0:RG])
            last.then_inc(s_ect, 1)
            pe.wait_ge(ready["carries_read"], 1)
            for q in range(2):
                last = pe.transpose(ps[0:RG, q * BK:q * BK + IT], car_t[:, q, :], ident[0:IT, 0:IT])
            last.then_inc(s_ect, 1)
            turn(IT, False)
            pe.wait_ge(ready["exp"], 1)
            add_tiles(main, 1, 1, "weighted")


_INS = ['x', 'src', 'dst', 'edge_attr_16', 'edge_type_8', 'L0_gnn_W', 'L0_gnn_b', 'L2_gnn_W_rel', 'L2_gnn_W_self_w',
        'L2_gnn_W_self_b', 'L3_gnn_W_lin', 'L3_gnn_W_edge', 'L3_gnn_att_src', 'L3_gnn_att_dst', 'L3_gnn_att_edge',
        'L3_gnn_bias', 'L3_gnn_ln_gamma', 'L3_gnn_ln_beta']
_OUTS = [((3125, 128), 'float32')]


def kernel(**inputs):
    import numpy as _np
    import concourse.bacc as _bacc
    from concourse import mybir as _mybir
    from concourse.bass_utils import run_bass_kernel_spmd as _run

    nc = _bacc.Bacc("TRN2", target_bir_lowering=False, num_devices=1)
    arrays, args = {}, []
    for name in _INS:
        a = _np.ascontiguousarray(inputs[name])
        arrays[f"in_{name}_dram"] = a
        args.append(nc.dram_tensor(f"in_{name}_dram", a.shape, _mybir.dt.from_np(a.dtype), kind="ExternalInput").ap())
    for i, (shape, dtype) in enumerate(_OUTS):
        dt = _mybir.dt.from_np(_np.dtype(dtype))
        args.append(nc.dram_tensor(f"out_{i}_dram", shape, dt, kind="ExternalOutput").ap())
    build(nc, *args)
    r = _run(nc, [arrays], core_ids=[0])
    got = tuple(r.results[0][f"out_{i}_dram"] for i in range(len(_OUTS)))
    return got[0]
```
